# Optimizing a Trainium2 kernel written in Bass

```python
import numpy as np
import jax
import jax.numpy as jnp

def _softmax(x, axis=-1):
    return jax.nn.softmax(x, axis=axis)

def _gelu(x):
    return jax.nn.gelu(x, approximate=True)

def _silu(x):
    return jax.nn.silu(x)

def _sigmoid(x):
    return jax.nn.sigmoid(x)

def _layernorm(x, axis=-1, eps=1e-05):
    m = jnp.mean(x, axis=axis, keepdims=True)
    v = jnp.var(x, axis=axis, keepdims=True)
    return (x - m) / jnp.sqrt(v + eps)

def _scatter_add(tgt, idx, src, axis=0):
    return tgt.at[idx].add(src)

def _segment_sum(src, seg, n):
    return jax.ops.segment_sum(src, seg, n)
kernel_name = 'mk_gnn_preln_d2_gnn_r8_95fdd9'

def setup_inputs(seed: int=0):
    np.random.seed(seed)
    _w = jnp.asarray

    def _rec_inputs():
        import jax
        import jax.numpy as jnp
        _gk = jax.random.key(seed)
        x = -0.000202 + 1 * jax.random.normal(jax.random.fold_in(_gk, 1), (6250, 128), jnp.float32)
        _s = jax.random.randint(jax.random.fold_in(_gk, 2), (50000,), 0, 6250, jnp.int32)
        _d = jax.random.randint(jax.random.fold_in(_gk, 3), (50000,), 0, 6250, jnp.int32)
        _loop = jnp.arange(6250, dtype=jnp.int32)
        src = jnp.concatenate([_s, _d, _loop])
        dst = jnp.concatenate([_d, _s, _loop])
        _o = jnp.argsort(dst, stable=True)
        src = src[_o]
        dst = dst[_o]
        edge_attr_128 = -5.16925e-05 + 1.00005 * jax.random.normal(jax.random.fold_in(_gk, 11), (106250, 128), jnp.float32)
        return (x, src, dst, edge_attr_128)
    x, src, dst, edge_attr_128 = _rec_inputs()

    def _L0_gnn_setup():
        import jax, jax.numpy as jnp
        import numpy as np
        N_NODES = 6250

        def _gcn_conv(x, W, b, src, dst, n_nodes):
            h = x @ W
            loop = jnp.arange(n_nodes, dtype=src.dtype)
            s = jnp.concatenate([src, loop])
            d = jnp.concatenate([dst, loop])
            ones = jnp.ones(s.shape[0], dtype=x.dtype)
            deg = jax.ops.segment_sum(ones, d, num_segments=n_nodes)
            dinv = jnp.where(deg > 0, jax.lax.rsqrt(deg), 0.0)
            norm = dinv[s] * dinv[d]
            msgs = h[s] * norm[:, None]
            out = jax.ops.segment_sum(msgs, d, num_segments=n_nodes)
            return out + b
        key = jax.random.key(seed)
        k1, k2, k3, k4 = jax.random.split(key, 4)
        in_ch, hid = (128, 128)
        x = jax.random.normal(k1, (N_NODES, in_ch), dtype=jnp.float32)
        edge_index = jax.random.randint(k2, (2, 100000), 0, N_NODES, dtype=jnp.int64)
        W1 = jax.random.normal(k3, (in_ch, hid), dtype=jnp.float32) / np.sqrt(in_ch)
        b1 = jnp.zeros((hid,), dtype=jnp.float32)
        W2 = jax.random.normal(k4, (hid, hid), dtype=jnp.float32) / np.sqrt(hid)
        b2 = jnp.zeros((hid,), dtype=jnp.float32)
        return {'x': x, 'edge_index': edge_index, 'W1': W1, 'b1': b1, 'W2': W2, 'b2': b2}
    _L0_gnn_all = _L0_gnn_setup()
    _L0_gnn_in = {k: v for k, v in _L0_gnn_all.items() if k in ('W1', 'b1', 'W2', 'b2')}
    del _L0_gnn_all

    def _L1_gnn_setup():
        import jax, jax.numpy as jnp
        import numpy as np
        N, E, D = (6250, 100000, 128)
        LN_EPS = 1e-05
        key = jax.random.key(seed)
        ks = jax.random.split(key, 8)
        x = jax.random.normal(ks[0], (N, D), dtype=jnp.float32)
        edge_index = jax.random.randint(ks[1], (2, E), 0, N, dtype=jnp.int64)
        edge_attr = jax.random.normal(ks[2], (E, D), dtype=jnp.float32)
        s_msg = 1.0 / np.sqrt(2 * D)
        s_upd = 1.0 / np.sqrt(2 * D)
        W_msg = jax.random.uniform(ks[3], (2 * D, D), jnp.float32, -s_msg, s_msg)
        b_msg = jax.random.uniform(ks[4], (D,), jnp.float32, -s_msg, s_msg)
        W_upd = jax.random.uniform(ks[5], (2 * D, D), jnp.float32, -s_upd, s_upd)
        b_upd = jax.random.uniform(ks[6], (D,), jnp.float32, -s_upd, s_upd)
        gamma = jnp.ones((D,), jnp.float32)
        beta = jnp.zeros((D,), jnp.float32)
        return {'x': x, 'edge_index': edge_index, 'edge_attr': edge_attr, 'W_msg': W_msg, 'b_msg': b_msg, 'W_upd': W_upd, 'b_upd': b_upd, 'gamma': gamma, 'beta': beta}
    _L1_gnn_all = _L1_gnn_setup()
    _L1_gnn_in = {k: v for k, v in _L1_gnn_all.items() if k in ('W_msg', 'b_msg', 'W_upd', 'b_upd', 'gamma', 'beta')}
    del _L1_gnn_all
    return {'x': x, 'src': src, 'dst': dst, 'edge_attr_128': edge_attr_128, 'L0_gnn_W1': _L0_gnn_in['W1'], 'L0_gnn_b1': _L0_gnn_in['b1'], 'L0_gnn_W2': _L0_gnn_in['W2'], 'L0_gnn_b2': _L0_gnn_in['b2'], 'L1_gnn_W_msg': _L1_gnn_in['W_msg'], 'L1_gnn_b_msg': _L1_gnn_in['b_msg'], 'L1_gnn_W_upd': _L1_gnn_in['W_upd'], 'L1_gnn_b_upd': _L1_gnn_in['b_upd'], 'L1_gnn_gamma': _L1_gnn_in['gamma'], 'L1_gnn_beta': _L1_gnn_in['beta']}

def reference(x, src, dst, edge_attr_128, L0_gnn_W1, L0_gnn_b1, L0_gnn_W2, L0_gnn_b2, L1_gnn_W_msg, L1_gnn_b_msg, L1_gnn_W_upd, L1_gnn_b_upd, L1_gnn_gamma, L1_gnn_beta):
    import jax
    import jax.numpy as jnp

    def _L0_gnn_ref(x, edge_index, W1, b1, W2, b2):
        import jax, jax.numpy as jnp
        import numpy as np
        N_NODES = 6250

        def _gcn_conv(x, W, b, src, dst, n_nodes):
            h = x @ W
            loop = jnp.arange(n_nodes, dtype=src.dtype)
            s = jnp.concatenate([src, loop])
            d = jnp.concatenate([dst, loop])
            ones = jnp.ones(s.shape[0], dtype=x.dtype)
            deg = jax.ops.segment_sum(ones, d, num_segments=n_nodes)
            dinv = jnp.where(deg > 0, jax.lax.rsqrt(deg), 0.0)
            norm = dinv[s] * dinv[d]
            msgs = h[s] * norm[:, None]
            out = jax.ops.segment_sum(msgs, d, num_segments=n_nodes)
            return out + b
        src, dst = (edge_index[0], edge_index[1])
        h = _gcn_conv(x, W1, b1, src, dst, N_NODES)
        h = jax.nn.relu(h)
        out = _gcn_conv(h, W2, b2, src, dst, N_NODES)
        return out

    def _L1_gnn_ref(x, edge_index, edge_attr, W_msg, b_msg, W_upd, b_upd, gamma, beta):
        import jax, jax.numpy as jnp
        import numpy as np
        N, E, D = (6250, 100000, 128)
        LN_EPS = 1e-05
        src, dst = (edge_index[0], edge_index[1])
        n = x.shape[0]
        msg_in = jnp.concatenate([x[src], edge_attr], axis=-1)
        msg = jax.nn.relu(msg_in @ W_msg + b_msg)
        summed = jax.ops.segment_sum(msg, dst, num_segments=n)
        counts = jax.ops.segment_sum(jnp.ones((msg.shape[0],), x.dtype), dst, num_segments=n)
        mean_msg = summed / jnp.maximum(counts, 1.0)[:, None]
        h = jnp.concatenate([x, mean_msg], axis=-1) @ W_upd + b_upd
        mu = jnp.mean(h, axis=-1, keepdims=True)
        var = jnp.mean(jnp.square(h - mu), axis=-1, keepdims=True)
        h = (h - mu) * jax.lax.rsqrt(var + LN_EPS) * gamma + beta
        return jax.nn.relu(h + x)
    edge_index = jnp.stack([src, dst])
    h = jnp.maximum(_layernorm(x, axis=-1), 0.0)
    x = x + _L0_gnn_ref(h, edge_index, L0_gnn_W1, L0_gnn_b1, L0_gnn_W2, L0_gnn_b2)
    h = jnp.maximum(_layernorm(x, axis=-1), 0.0)
    x = x + _L1_gnn_ref(h, edge_index, edge_attr_128, L1_gnn_W_msg, L1_gnn_b_msg, L1_gnn_W_upd, L1_gnn_b_upd, L1_gnn_gamma, L1_gnn_beta)
    return x

_drawn_inputs = setup_inputs


def setup_inputs(seed=0):
    import zlib

    import numpy as np

    out = dict(_drawn_inputs(seed))
    spreads = {'L0_gnn_b1': (0.0, 0.1),
     'L0_gnn_b2': (0.0, 0.1),
     'L1_gnn_gamma': (1.0, 0.2),
     'L1_gnn_beta': (0.0, 0.1)}
    factors = {'L1_gnn_b_msg': 5.108}
    for name, (base, spread) in spreads.items():
        noise = np.random.default_rng([zlib.crc32(name.encode()), seed]).standard_normal(out[name].shape)
        drawn = base * np.exp(spread * noise) if base else spread * noise
        out[name] = jnp.asarray(drawn.astype(out[name].dtype))
    for name, factor in factors.items():
        out[name] = (out[name] * factor).astype(out[name].dtype)
    return out
```

```python
import concourse.bass as bass
from concourse import mybir
from contextlib import ExitStack

P = 128
TILES = 8
W = 96
RING = 4
CB = 4
CH = CB * P
HT = 16
PAD_DST = 16384
PAD_LIMIT = 8192
EPS = 1e-5


def gnn_program(nc, x, src, dst, edge, W1, b1, W2, b2, W_msg, b_msg, W_upd, b_upd, gamma, beta, out):
    f32, i32, bf16 = mybir.dt.float32, mybir.dt.int32, mybir.dt.bfloat16
    ALU, ACT, AX = mybir.AluOpType, mybir.ActivationFunctionType, mybir.AxisListType

    N = x.shape[0]
    E = src.shape[0]
    SE = P * TILES
    NS = -(-E // (SE * RING)) * RING
    FULL = E // SE
    LAST = E - FULL * SE
    assert NS == FULL + 1 and LAST > 0 and NS <= P
    BODIES = NS // RING
    NCH = -(-N // CH)
    NB = NCH * CB
    NP = NB * P
    assert NCH % 2 == 1 and NCH >= 5
    XB = N // P
    XR = N - XB * P
    HI = -(-N // P)
    NW = -(-N // W)
    assert NW * W <= NP and N - 1 + W <= NP and N < PAD_LIMIT
    GROUPS = NS * TILES // HT
    assert GROUPS % 2 == 0 and GROUPS >= 6

    table = nc.dram_tensor("table", (NP, P), f32, kind="Internal").ap()

    ctx = ExitStack()
    with ctx:
        def sb(name, shape, dt=f32):
            return ctx.enter_context(nc.sbuf_tensor(name, shape, dt))

        def sem(name):
            return ctx.enter_context(nc.semaphore(name))

        w1 = sb("w1", [P, P])
        w2 = sb("w2", [P, P])
        w_node = sb("w_node", [P, 2 * P])
        w_edge = sb("w_edge", [P, P])
        w_mean = sb("w_mean", [P, P])
        b1_col = sb("b1_col", [P, 1])
        b2_bc = sb("b2_bc", [P, P])
        bmsg_bc = sb("bmsg_bc", [P, P])
        bupd_bc = sb("bupd_bc", [P, P])
        gamma_bc = sb("gamma_bc", [P, P])
        beta_bc = sb("beta_bc", [P, P])
        ident = sb("ident", [P, P])
        ones = sb("ones", [P, P])
        zeros = sb("zeros", [P, CH])
        iota_i = sb("iota_i", [P, P], i32)
        iota_w = sb("iota_w", [P, W])
        window_i = sb("window_i", [P, NW], i32)
        window_off = sb("window_off", [P, NW])
        eps_col = sb("eps_col", [P, 1])

        src_col = sb("src_col", [P, NS, TILES], i32)
        rel_col = sb("rel_col", [P, NS, TILES])
        dst_col = sb("dst_col", [P, NS, TILES], i32)
        part_i = sb("part_i", [P, NS, TILES], i32)
        lo_col = sb("lo_col", [P, NS * TILES], bf16)
        hi_col = sb("hi_col", [P, NS * TILES], bf16)
        base_span = sb("base_span", [NS, 2])
        base_row_f = sb("base_row_f", [1, NS])
        base_row = sb("base_row", [1, NS], i32)
        span_max = sb("span_max", [1, 1])
        is_banded = sb("is_banded", [1, 1])
        nwin_f = sb("nwin_f", [1, 1])
        nwin_i = sb("nwin_i", [1, 1], i32)
        banded_col = sb("banded_col", [NS, 1])
        base_used = sb("base_used", [NS, 1])

        x_sb = sb("x_sb", [P, NB, P])
        acc = sb("acc", [P, NP])
        dinv_bc = sb("dinv_bc", [P, NP])
        node_u = sb("node_u", [P, NB, P])
        hb_all = dinv_bc[:, :].rearrange("p (b f) -> p b f", f=P)
        count = sb("count", [P, NB])
        dinv = sb("dinv", [P, NB])
        rcount = sb("rcount", [P, NB])
        mv = sb("mv", [P, NB, 2])
        rstd = sb("rstd", [P, NB])
        nmr = sb("nmr", [P, NB])

        acc_bf = acc[:, :].bitcast(bf16)
        iota_hist = acc_bf[:, 0:P * HT].rearrange("p (v t) -> p v t", t=HT)
        oh_lo = acc_bf[:, P * HT:3 * P * HT].rearrange("p (h v t) -> p h v t", h=2, t=HT)
        oh_hi = acc_bf[:, 3 * P * HT:(3 * P + 2 * HI) * HT].rearrange("p (h v t) -> p h v t", h=2, t=HT)

        G = sb("G", [P, RING, TILES, P])
        dst_rows, src_rows, dst_f, src_f = [G[0:NS, u].rearrange("s j f -> s (j f)") for u in range(4)]
        dst_rows, src_rows = dst_rows.bitcast(i32), src_rows.bitcast(i32)
        edges = sb("edges", [P, RING, TILES, P])
        idx_ring = sb("idx_ring", [P, RING, TILES], i32)
        edgeT = sb("edgeT", [P, 2, CH])
        oh = sb("oh", [P, TILES, W])
        z = sb("z", [P, 2, CH])
        st = sb("st", [P, 2, CH])
        hT = sb("hT", [P, 2, CH])
        y = sb("y", [P, 2, CH])
        stats = sb("stats", [P, 2, CB, 6])
        cmv = sb("cmv", [P, 2, CB, 2])
        cstd = sb("cstd", [P, 2, CB])
        crstd = sb("crstd", [P, 2, CB])
        cnmr = sb("cnmr", [P, 2, CB])

        banks = [ctx.enter_context(nc.psum_tensor(f"bank{i}", [P, 512], f32)) for i in range(8)]

        s_loads = sem("s_loads")
        s_x = sem("s_x")
        s_idx = sem("s_idx")
        s_pool0 = sem("s_pool0")
        s_dve0 = sem("s_dve0")
        s_pad = sem("s_pad")
        s_idxT = sem("s_idxT")
        s_base = sem("s_base")
        s_band = sem("s_band")
        s_relT = sem("s_relT")
        s_hist = sem("s_hist")
        s_histmm = sem("s_histmm")
        s_std = sem("s_std")
        s_rstd = sem("s_rstd")
        s_sdeg = sem("s_sdeg")
        s_h = sem("s_h")
        s_hTp = sem("s_hTp")
        s_hTc = sem("s_hTc")
        s_hw = sem("s_hw")
        s_u = sem("s_u")
        s_t1 = sem("s_t1")
        s_tab = [sem(f"s_tab{h}") for h in range(2)]
        s_selfT = sem("s_selfT")
        s_acc0 = sem("s_acc0")
        s_diag = sem("s_diag")
        s_dbc = sem("s_dbc")
        s_dbcc = sem("s_dbcc")
        s_xb = sem("s_xb")
        s_idxr = sem("s_idxr")
        s_g = [sem(f"s_g{u}") for u in range(RING)]
        s_free = sem("s_free")
        s_oh = sem("s_oh")
        s_agg = sem("s_agg")
        s_added = sem("s_added")
        s_z = sem("s_z")
        s_zr = sem("s_zr")
        s_zw = sem("s_zw")
        s_t = sem("s_t")
        s_c = {n: sem("s_c_" + n) for n in
               ("z", "tr", "zero", "x2", "bn", "std", "rstd", "h", "hT", "hTc", "hw", "t3", "u", "hb")}
        s_ub = sem("s_ub")
        s_started_pool = sem("s_started_pool")
        s_started_pe = sem("s_started_pe")
        s_started_dve = sem("s_started_dve")
        s_bnall = sem("s_bnall")
        s_bn1 = sem("s_bn1")
        s_degree = sem("s_degree")
        s_srccol = sem("s_srccol")
        s_dstcol = sem("s_dstcol")
        s_split = sem("s_split")
        s_iota = sem("s_iota")
        s_red = sem("s_red")
        s_span = sem("s_span")
        s_small = sem("s_small")
        s_flag = sem("s_flag")
        s_rel = sem("s_rel")
        s_relcol = sem("s_relcol")
        s_own = sem("s_own")
        s_e = [sem(f"s_e{u}") for u in range(RING)]
        s_eT = sem("s_eT")
        s_eTc = sem("s_eTc")
        s_m = sem("s_m")
        s_msum = sem("s_msum")
        s_msg = sem("s_msg")
        s_d = {n: sem("s_d_" + n) for n in
               ("z", "mm", "y1", "y", "bn", "std", "rstd", "n", "g", "b", "fin")}
        s_out = [sem(f"s_out{h}") for h in range(2)]

        block = ctx.enter_context(nc.Block())

        def bc_free(ap, n):
            return ap.rearrange("p (k o) -> p k o", o=1).to_broadcast([ap.shape[0], ap.shape[1], n])

        def bc_mid(ap, k):
            return ap.rearrange("p (o n) -> p o n", o=1).to_broadcast([ap.shape[0], k, ap.shape[1]])

        def cols(ap, c):
            return ap[:, bass.ds(c * CH, CH)]

        def blk(ap, c):
            return ap[:, bass.ds(c * CB, CB)]

        def q3(ap):
            return ap.rearrange("p (k f) -> p k f", f=P)

        def chunks(eng, step):
            for c in range(3):
                step(c, c, c % 2, c // 2)
            with eng.Fori(1, (NCH - 1) // 2) as i:
                step(2 * i + 1, 3, 1, i)
                step(2 * i + 2, 4, 0, i + 1)

        def bodies(eng, step):
            step(0, True, False)
            with eng.Fori(1, BODIES - 1) as i:
                step(i, False, False)
            step(BODIES - 1, False, True)

        def counter(eng, started):
            return lambda: eng.sem_inc(started, 1)

        def table_chunk(c):
            return table[bass.ds(c * CH, CH), :].rearrange("(k p) f -> p k f", p=P)

        STORES = [16 * (NCH - NCH // 2), 16 * (NCH // 2)]
        N_WEIGHTS = 6
        N_BIASES = 6

        @block.sync
        def _(sp):
            sp.wait_ge(s_pad, 1)
            rows = FULL * SE
            sp.dma_start(dst_rows[0:FULL, :], dst[0:rows].rearrange("(s e) -> s e", e=SE)).then_inc(s_idx, 16)
            sp.dma_start(dst_rows[FULL:NS, SE - LAST:SE], dst[rows:E].rearrange("(s e) -> s e", s=1)).then_inc(s_idx, 16)
            sp.dma_start(src_rows[0:FULL, :], src[0:rows].rearrange("(s e) -> s e", e=SE)).then_inc(s_idx, 16)
            sp.dma_start(src_rows[FULL:NS, :], src[E - SE:E].rearrange("(s e) -> s e", s=1)).then_inc(s_idx, 16)
            sp.wait_ge(s_pad, 2)
            sp.dma_start(x_sb[:, 0:XB, :], x[0:XB * P, :].rearrange("(b p) f -> p b f", p=P)).then_inc(s_x, 16)
            sp.dma_start(x_sb[0:XR, XB, :], x[XB * P:N, :]).then_inc(s_x, 16)

            def load_edges(i, u, row, wait):
                if wait:
                    sp.wait_ge(s_eT, 2 * RING * i - 2 * RING + 2 * u + 2)
                sp.dma_start(edges[:, u, :, :].rearrange("p j f -> p (j f)"),
                             edge[row, :].rearrange("(p j) f -> p (j f)", p=P)).then_inc(s_e[u], 16)

            for u in range(RING):
                load_edges(0, u, slice(u * SE, (u + 1) * SE), False)

            def store_scaled(c, n, h, m):
                sp.wait_ge(s_t1, c + 1)
                sp.dma_start(table_chunk(c), blk(node_u, c)).then_inc(s_tab[h], 16)
            chunks(sp, store_scaled)

            def store_second(c, n, h, m):
                sp.wait_ge(s_t, c + 1)
                sp.dma_start(table_chunk(c), q3(st[:, h])).then_inc(s_tab[h], 16)
            chunks(sp, store_second)

            def store_third(c, n, h, m):
                sp.wait_ge(s_c["t3"], c + 1)
                sp.dma_start(table_chunk(c), q3(st[:, h])).then_inc(s_tab[h], 16)
            chunks(sp, store_third)

            with sp.Fori(1, BODIES - 1) as i:
                for u in range(RING):
                    load_edges(i, u, bass.ds(i * (RING * SE) + u * SE, SE), True)
            i = BODIES - 1
            for u in range(RING):
                s = i * RING + u
                row = min(s * SE, E - SE)
                load_edges(i, u, slice(row, row + SE), True)

            def store_out(c, n, h, m):
                sp.wait_ge(s_d["fin"], c + 1)
                sp.dma_start(out[bass.ds(c * CH, CH), :].rearrange("(k p) f -> p k f", p=P),
                             q3(y[:, h])).then_inc(s_out[h], 16)
            for c in range(3):
                store_out(c, c, c % 2, 0)
            whole = N // CH
            pairs = (whole - 3) // 2
            with sp.Fori(1, pairs + 1) as i:
                store_out(2 * i + 1, 3, 1, i)
                store_out(2 * i + 2, 4, 0, i)
            for c in range(3 + 2 * pairs, whole):
                store_out(c, c, c % 2, 0)
            stores = [whole - whole // 2, whole // 2]
            if N > whole * CH:
                sp.wait_ge(s_d["fin"], whole + 1)
                tail = q3(y[:, whole % 2])
                for b in range(whole * CB, HI):
                    n = min(P, N - b * P)
                    sp.dma_start(out[b * P:b * P + n, :], tail[0:n, b - whole * CB, :]).then_inc(s_out[whole % 2], 16)
                    stores[whole % 2] += 1
            for h in range(2):
                sp.wait_ge(s_out[h], 16 * stores[h])

        @block.gpsimd
        def _(pool):
            pool.memset(dst_rows[:, :], PAD_DST).then_inc(s_pad, 1)
            pool.memset(x_sb[:, XB:NB, :], 0.0).then_inc(s_pad, 1)
            pool.memset(ident[:, :], 0.0).then_inc(s_pool0, 1)
            pool.wait_ge(s_pool0, 1)
            pool.affine_select(out=ident[:, :], in_=ident[:, :], compare_op=ALU.not_equal, fill=1.0,
                               base=0, pattern=[[-1, P]], channel_multiplier=1).then_inc(s_pool0, 1)
            pool.iota(iota_i[:, :], pattern=[[1, P]], base=0, channel_multiplier=0).then_inc(s_pool0, 1)
            pool.iota(window_i[:, :], pattern=[[W, NW]], base=0, channel_multiplier=0).then_inc(s_pool0, 1)
            pool.memset(ones[:, :], 1.0).then_inc(s_pool0, 1)
            pool.memset(zeros[:, :], 0.0).then_inc(s_pool0, 1)
            pool.memset(eps_col[:, :], EPS).then_inc(s_pool0, 1)

            next_supertile = counter(pool, s_started_pool)

            def gather_phase(ph):
                def body(i, first, last):
                    for u in range(RING):
                        if not (ph == 0 and first):
                            pool.wait_ge(s_free, RING * i + (ph * NS + u - RING + 1))
                        pool.wait_ge(s_idxr, RING * i + (ph * NS + u + 1))
                        for h in range(2):
                            pool.wait_ge(s_tab[h], STORES[h] * (ph + 1))
                        next_supertile()
                        for j in range(TILES):
                            pool.indirect_dma_start(
                                out=G[:, u, j, :], out_offset=None, in_=table,
                                in_offset=bass.IndirectOffsetOnAxis(ap=idx_ring[:, u, j:j + 1], axis=0),
                            ).then_inc(s_g[u], 16)
                bodies(pool, body)

            gather_phase(0)
            gather_phase(1)

            def third_table(c, n, h, m):
                if n == 0:
                    pool.wait_ge(s_free, 2 * NS)
                if n >= 2:
                    pool.wait_ge(s_c["tr"], c - 1)
                pool.tensor_tensor(z[:, h], cols(acc, c), cols(dinv_bc, c), ALU.mult).then_inc(s_c["z"], 1)
                if n >= 1:
                    keep_h(c - 1, 1 - h)

            def keep_h(c, h):
                pool.wait_ge(s_c["h"], c + 1)
                pool.wait_ge(s_c["z"], c + 1)
                pool.tensor_tensor(blk(hb_all, c), q3(hst[:, h]), bc_mid(beta_bc[:, :], CB),
                                   ALU.add).then_inc(s_c["hb"], 1)
            hst = y
            pool.wait_ge(s_loads, 16 * (N_WEIGHTS + N_BIASES))
            chunks(pool, third_table)
            keep_h(NCH - 1, (NCH - 1) % 2)

            gather_phase(2)

            def times_gamma(c, n, h, m):
                pool.wait_ge(s_d["n"], c + 1)
                pool.tensor_tensor(q3(st[:, h]), q3(st[:, h]), bc_mid(gamma_bc[:, :], CB),
                                   ALU.mult).then_inc(s_d["g"], 1)
            chunks(pool, times_gamma)

        @block.scalar
        def _(act):
            for dram, tile in ((W1, w1[:, :]), (W2, w2[:, :]),
                               (W_msg[0:P, :], w_node[:, 0:P]), (W_upd[0:P, :], w_node[:, P:2 * P]),
                               (W_msg[P:2 * P, :], w_edge[:, :]), (W_upd[P:2 * P, :], w_mean[:, :])):
                act.dma_start(tile, dram).then_inc(s_loads, 16)
            act.dma_start(b1_col[:, :], b1.rearrange("(p o) -> p o", o=1)).then_inc(s_loads, 16)
            for dram, tile in ((b2, b2_bc), (b_msg, bmsg_bc), (b_upd, bupd_bc), (gamma, gamma_bc), (beta, beta_bc)):
                act.dma_start(tile[:, :], dram.rearrange("(o f) -> o f", o=1).to_broadcast([P, P])).then_inc(s_loads, 16)

            act.wait_ge(s_pool0, 7)
            act.wait_ge(s_bnall, 1)
            act.activation(rstd[:, :], mv[:, :, 1], ACT.Sqrt, bias=eps_col[:, 0:1]).then_inc(s_std, 1)
            act.wait_ge(s_rstd, 1)

            def first_h(c, n, h, m):
                if n >= 2:
                    act.wait_ge(s_hTp, c - 1)
                for k in range(CB):
                    last = act.activation(z[:, h, k * P:(k + 1) * P], x_sb[:, c * CB + k, :], ACT.Relu,
                                          scale=rstd[:, bass.ds(c * CB + k, 1)], bias=nmr[:, bass.ds(c * CB + k, 1)])
                last.then_inc(s_h, 1)
                if n >= 1:
                    copy_hw(c - 1, n - 1, 1 - h, m - (1 - h))
                act.wait_ge(s_hTp, c + 1)
                act.activation(hT[:, h], banks[h][:, :], ACT.Copy).then_inc(s_hTc, 1)

            def copy_hw(c, n, h, m):
                act.wait_ge(s_hw, c + 1)
                act.activation(blk(node_u, c), q3(banks[2 + h][:, :]), ACT.Copy).then_inc(s_u, 1)
            chunks(act, first_h)
            copy_hw(NCH - 1, 9, (NCH - 1) % 2, (NCH - 1) // 2)

            act.wait_ge(s_degree, 1)
            act.activation(dinv[:, :], count[:, :], ACT.Sqrt, bias=ones[:, 0:1]).then_inc(s_sdeg, 1)

            def fill_indices(ph, i, u, first):
                if not (ph == 0 and first):
                    act.wait_ge(s_g[u], 16 * TILES * i + 16 * TILES * BODIES * ph)
                act.activation(idx_ring[:, u, :], src_col[:, RING * i + u, :], ACT.Copy).then_inc(s_idxr, 1)

            act.wait_ge(s_srccol, 1)
            fill_indices(0, 0, 0, True)
            fill_indices(0, 0, 1, True)

            def own_rows(c, n, h, m):
                act.wait_ge(s_selfT, c + 1)
                act.activation(cols(acc, c), banks[h][:, :], ACT.Copy).then_inc(s_acc0, 1)
            chunks(act, own_rows)

            def dinv_rows(c, n, h, m):
                act.wait_ge(s_dbc, c + 1)
                act.activation(cols(dinv_bc, c), banks[2 + h][:, :], ACT.Copy).then_inc(s_dbcc, 1)
            chunks(act, dinv_rows)

            def gcn_phase(ph):
                if ph:
                    fill_indices(ph, 0, 0, True)
                    fill_indices(ph, 0, 1, True)

                def body(i, first, last):
                    for u in range(RING):
                        if not (last and u >= RING - 2):
                            fill_indices(ph, i if u < 2 else i + 1, (u + 2) % RING, first and u < 2)
                bodies(act, body)
            gcn_phase(0)

            def second_z(c, n, h, m):
                act.wait_ge(s_z, c + 1)
                act.activation(z[:, h], z[:, h], ACT.Relu, bias=b1_col[:, 0:1]).then_inc(s_zr, 1)
                if n >= 1:
                    second_own(c - 1, 1 - h)

            def second_own(c, h):
                act.wait_ge(s_selfT, NCH + c + 1)
                act.activation(cols(acc, c), banks[2 + h][:, :], ACT.Copy).then_inc(s_acc0, 1)
            chunks(act, second_z)
            second_own(NCH - 1, (NCH - 1) % 2)
            gcn_phase(1)

            def third_std(c, n, h, m):
                act.wait_ge(s_c["bn"], 2 * CB * c + 2 * CB)
                act.activation(cstd[:, h], cmv[:, h, :, 1], ACT.Sqrt, bias=eps_col[:, 0:1]).then_inc(s_c["std"], 1)
                if n >= 1:
                    third_rest(c - 1, n - 1, 1 - h, m - (1 - h))

            def third_rest(c, n, h, m):
                act.wait_ge(s_c["rstd"], 2 * c + 2)
                if n >= 2:
                    act.wait_ge(s_c["hT"], c - 1)
                    act.wait_ge(s_c["hb"], c - 1)
                for k in range(CB):
                    last = act.activation(y[:, h, k * P:(k + 1) * P], x_sb[:, c * CB + k, :], ACT.Relu,
                                          scale=crstd[:, h, k:k + 1], bias=cnmr[:, h, k:k + 1])
                last.then_inc(s_c["h"], 1)
                act.wait_ge(s_c["tr"], c + 1)
                act.activation(cols(acc, c), zeros[:, :], ACT.Copy).then_inc(s_acc0, 1)
                act.wait_ge(s_c["hT"], c + 1)
                act.activation(hT[:, h], banks[2][:, :], ACT.Copy).then_inc(s_c["hTc"], 1)
                act.wait_ge(s_c["hw"], 2 * c + 2)
                act.activation(blk(node_u, c), q3(banks[5][:, :]), ACT.Copy).then_inc(s_c["u"], 1)
            chunks(act, third_std)
            third_rest(NCH - 1, 9, (NCH - 1) % 2, (NCH - 1) // 2)

            def copy_edges(i, u, first):
                for half in range(2):
                    n = 2 * RING * i + 2 * u + half
                    act.wait_ge(s_eT, n + 1)
                    if not first:
                        act.wait_ge(s_m, n - 1)
                    act.activation(edgeT[:, half], banks[half][:, :], ACT.Copy).then_inc(s_eTc, 1)

            fill_indices(2, 0, 0, True)
            fill_indices(2, 0, 1, True)
            copy_edges(0, 0, True)

            def message_body(i, first, last):
                for u in range(RING):
                    if not (last and u == RING - 1):
                        copy_edges(i if u < RING - 1 else i + 1, (u + 1) % RING, False)
                    if not (last and u >= RING - 2):
                        fill_indices(2, i if u < 2 else i + 1, (u + 2) % RING, False)
                    for half in range(2):
                        act.wait_ge(s_msum, 2 * RING * i + 2 * u + half + 1)
                        act.activation(G[:, u, 4 * half:4 * half + 4, :], G[:, u, 4 * half:4 * half + 4, :],
                                       ACT.Relu).then_inc(s_msg, 1)
            bodies(act, message_body)

            def end_z(c, n, h, m):
                if n == 0:
                    act.wait_ge(s_free, 3 * NS)
                if n >= 2:
                    act.wait_ge(s_d["mm"], c - 1)
                act.activation(z[:, h], cols(acc, c), ACT.Copy).then_inc(s_d["z"], 1)
                if n >= 1:
                    end_norm(c - 1, n - 1, 1 - h, m - (1 - h))

            def end_norm(c, n, h, m):
                act.wait_ge(s_d["bn"], 2 * CB * c + 2 * CB)
                act.activation(cstd[:, h], cmv[:, h, :, 1], ACT.Sqrt, bias=eps_col[:, 0:1]).then_inc(s_d["std"], 1)
                act.wait_ge(s_d["rstd"], 2 * c + 2)
                if n >= 2:
                    act.wait_ge(s_d["b"], c - 1)
                for k in range(CB):
                    last = act.activation(st[:, h, k * P:(k + 1) * P], hT[:, h, k * P:(k + 1) * P], ACT.Identity,
                                          scale=crstd[:, h, k:k + 1], bias=cnmr[:, h, k:k + 1])
                last.then_inc(s_d["n"], 1)
            chunks(act, end_z)
            end_norm(NCH - 1, 9, (NCH - 1) % 2, (NCH - 1) // 2)

        @block.tensor
        def _(pe):
            pe.wait_ge(s_pool0, 7)
            pe.wait_ge(s_dve0, 1)
            for j in range(TILES):
                last = pe.transpose(banks[j // 4][:, (j % 4) * P:(j % 4) * P + NS],
                                    dst_f[:, :].rearrange("s (p j) -> s p j", j=TILES)[:, :, j],
                                    ident[0:NS, 0:NS])
            last.then_inc(s_idxT, 1)
            pe.wait_ge(s_dve0, 2)
            for j in range(TILES):
                last = pe.transpose(banks[2 + j // 4][:, (j % 4) * P:(j % 4) * P + NS],
                                    src_f[:, :].rearrange("s (p j) -> s p j", j=TILES)[:, :, j],
                                    ident[0:NS, 0:NS])
            last.then_inc(s_idxT, 1)
            pe.wait_ge(s_span, 1)
            pe.transpose(banks[4][0:1, 0:NS], base_span[:, 0:1], ident[0:NS, 0:NS])
            pe.transpose(banks[4][0:1, P:P + NS], base_span[:, 1:2], ident[0:NS, 0:NS]).then_inc(s_base, 1)
            pe.wait_ge(s_flag, 1)
            pe.matmul(banks[5][0:NS, 0:1], ones[0:1, 0:NS], is_banded[0:1, 0:1], start=True, stop=True).then_inc(s_band, 1)
            pe.wait_ge(s_rel, 1)
            for j in range(TILES):
                last = pe.transpose(banks[4 + j // 4][:, (j % 4) * P:(j % 4) * P + NS],
                                    dst_f[:, :].rearrange("s (p j) -> s p j", j=TILES)[:, :, j],
                                    ident[0:NS, 0:NS])
            last.then_inc(s_relT, 1)

            def hist(g, h, start, stop):
                pe.wait_ge(s_hist, g + 1)
                for t in range(HT):
                    last = pe.matmul(banks[7][:, 0:HI], oh_lo[:, h, :, t], oh_hi[:, h, :, t],
                                     start=start and t == 0, stop=stop and t == HT - 1)
                last.then_inc(s_histmm, 1)

            def first_products(c, n, h, m):
                pe.wait_ge(s_h, c + 1)
                if n == 0:
                    pe.wait_ge(s_dstcol, 1)
                    pe.wait_ge(s_srccol, 1)
                if n >= 2:
                    pe.wait_ge(s_hTc, c - 1)
                for k in range(CB):
                    last = pe.transpose(banks[h][:, k * P:(k + 1) * P], z[:, h, k * P:(k + 1) * P], ident[:, :])
                last.then_inc(s_hTp, 1)
                pe.wait_ge(s_hTc, c + 1)
                if n >= 2:
                    pe.wait_ge(s_u, c - 1)
                for k in range(CB):
                    last = pe.matmul(banks[2 + h][:, k * P:(k + 1) * P], hT[:, h, k * P:(k + 1) * P], w1[:, :],
                                     start=True, stop=True)
                last.then_inc(s_hw, 1)

            pe.wait_ge(s_loads, 16 * (N_WEIGHTS + N_BIASES))
            hist(0, 0, True, False)
            hist(1, 1, False, False)
            side = min(NCH, 3)
            for c in range(3):
                first_products(c, c, c % 2, 0)
            PAIRS = GROUPS // 2
            inner = (NCH - 3) // 2
            assert PAIRS - 2 >= inner
            with pe.Fori(1, inner + 1) as i:
                hist(2 * i, 0, False, False)
                first_products(2 * i + 1, 3, 1, i)
                hist(2 * i + 1, 1, False, False)
                first_products(2 * i + 2, 4, 0, i)
            with pe.Fori(inner + 1, PAIRS - 1) as i:
                hist(2 * i, 0, False, False)
                hist(2 * i + 1, 1, False, False)
            hist(GROUPS - 2, 0, False, False)
            hist(GROUPS - 1, 1, False, True)

            def own_rows(c, n, h, m):
                pe.wait_ge(s_own, c + 1)
                if n == 0:
                    pe.wait_ge(s_u, NCH)
                if n >= 2:
                    pe.wait_ge(s_acc0, c - 1)
                for k in range(CB):
                    last = pe.transpose(banks[h][:, k * P:(k + 1) * P], st[:, h, k * P:(k + 1) * P], ident[:, :])
                last.then_inc(s_selfT, 1)
            chunks(pe, own_rows)

            def dinv_rows(c, n, h, m):
                pe.wait_ge(s_diag, c + 1)
                if n >= 2:
                    pe.wait_ge(s_dbcc, c - 1)
                pe.matmul(banks[2 + h][:, :], ones[:, :], z[:, h], start=True, stop=True).then_inc(s_dbc, 1)
            chunks(pe, dinv_rows)

            nwin = pe.value_load(nwin_i[0:1, 0:1], min_val=1, max_val=NW)
            next_supertile = counter(pe, s_started_pe)
            done = pe.alloc_register("windows_pe")
            pe.reg_mov(done, 0)

            def sum_supertile(u):
                next_supertile()
                with pe.Fori(0, nwin):
                    pe.reg_add(done, done, 1)
                    d = pe.snap(done)
                    pe.wait_ge(s_oh, d)
                    for j in range(TILES):
                        last = pe.matmul(banks[6][:, 0:W], G[:, u, j, :], oh[:, j, :], start=j == 0, stop=j == TILES - 1)
                    last.then_inc(s_agg, 1)

            def gcn_phase(ph):
                with pe.Fori(0, BODIES) as i:
                    for u in range(RING):
                        pe.wait_ge(s_g[u], 16 * TILES * i + 16 * TILES * (BODIES * ph + 1))
                        sum_supertile(u)
            gcn_phase(0)

            def second_table(c, n, h, m):
                pe.wait_ge(s_zr, c + 1)
                if n >= 2:
                    pe.wait_ge(s_t, c - 1)
                for k in range(CB):
                    last = pe.matmul(banks[h][:, k * P:(k + 1) * P], z[:, h, k * P:(k + 1) * P], w2[:, :],
                                     start=True, stop=True)
                last.then_inc(s_zw, 1)
                if n >= 1:
                    second_own(c - 1, n - 1, 1 - h, m - (1 - h))

            def second_own(c, n, h, m):
                pe.wait_ge(s_t, c + 1)
                if n >= 2:
                    pe.wait_ge(s_acc0, NCH + c - 1)
                for k in range(CB):
                    last = pe.transpose(banks[2 + h][:, k * P:(k + 1) * P], st[:, h, k * P:(k + 1) * P], ident[:, :])
                last.then_inc(s_selfT, 1)
            chunks(pe, second_table)
            second_own(NCH - 1, 9, (NCH - 1) % 2, (NCH - 1) // 2)
            gcn_phase(1)

            def third_tr(c, n, h, m):
                pe.wait_ge(s_c["z"], c + 1)
                if n >= 2:
                    pe.wait_ge(s_c["x2"], c - 1)
                for k in range(CB):
                    last = pe.transpose(banks[h][:, k * P:(k + 1) * P], z[:, h, k * P:(k + 1) * P], ident[:, :])
                last.then_inc(s_c["tr"], 1)
                if n >= 1:
                    third_products(c - 1, n - 1, 1 - h, m - (1 - h))

            def third_products(c, n, h, m):
                pe.wait_ge(s_c["h"], c + 1)
                if n >= 1:
                    pe.wait_ge(s_c["hTc"], c)
                for k in range(CB):
                    last = pe.transpose(banks[2][:, k * P:(k + 1) * P], y[:, h, k * P:(k + 1) * P], ident[:, :])
                last.then_inc(s_c["hT"], 1)
                pe.wait_ge(s_c["hTc"], c + 1)
                if n >= 1:
                    pe.wait_ge(s_c["t3"], c)
                    pe.wait_ge(s_c["u"], c)
                for g in range(2):
                    for k in range(CB):
                        last = pe.matmul(banks[4 + g][:, k * P:(k + 1) * P], hT[:, h, k * P:(k + 1) * P],
                                         w_node[:, g * P:(g + 1) * P], start=True, stop=True)
                    last.then_inc(s_c["hw"], 1)
            chunks(pe, third_tr)
            third_products(NCH - 1, 9, (NCH - 1) % 2, (NCH - 1) // 2)

            def transpose_edges(i, u, n):
                pe.wait_ge(s_e[u], 16 * i + 16)
                for half in range(2):
                    if n >= 1:
                        pe.wait_ge(s_eTc, 2 * RING * i + 2 * u + half - 1)
                    for k in range(4):
                        last = pe.transpose(banks[half][:, k * P:(k + 1) * P], edges[:, u, 4 * half + k, :], ident[:, :])
                    last.then_inc(s_eT, 1)

            def edge_products(i, u, n):
                for half in range(2):
                    m = 2 * RING * i + 2 * u + half
                    pe.wait_ge(s_eTc, m + 1)
                    if n >= 2:
                        pe.wait_ge(s_msum, m - 3)
                    for k in range(4):
                        last = pe.matmul(banks[2 + 2 * (u % 2) + half][:, k * P:(k + 1) * P],
                                         edgeT[:, half, k * P:(k + 1) * P], w_edge[:, :], start=True, stop=True)
                    last.then_inc(s_m, 1)

            pe.wait_ge(s_c["t3"], NCH)
            pe.wait_ge(s_c["u"], NCH)
            transpose_edges(0, 0, 0)
            edge_products(0, 0, 0)

            def message_body(i, first, last):
                for u in range(RING):
                    if not (last and u == RING - 1):
                        nxt = (i if u < RING - 1 else i + 1, (u + 1) % RING)
                        n = u + 1 if first else 9
                        transpose_edges(*nxt, n)
                        edge_products(*nxt, n)
                    pe.wait_ge(s_msg, 2 * RING * i + 2 * u + 2)
                    sum_supertile(u)
            bodies(pe, message_body)

            def end_products(c, n, h, m):
                pe.wait_ge(s_d["z"], c + 1)
                if n >= 2:
                    pe.wait_ge(s_d["y1"], c - 1)
                for k in range(CB):
                    last = pe.matmul(banks[h][:, k * P:(k + 1) * P], z[:, h, k * P:(k + 1) * P], w_mean[:, :],
                                     start=True, stop=True)
                last.then_inc(s_d["mm"], 1)
            chunks(pe, end_products)

        @block.vector
        def _(dve):
            next_norm = counter(dve, s_started_dve)
            dve.wait_ge(s_idx, 64)
            dve.tensor_copy(dst_f[:, :], dst_rows[:, :]).then_inc(s_dve0, 1)
            dve.tensor_copy(src_f[:, :], src_rows[:, :]).then_inc(s_dve0, 1)
            dve.wait_ge(s_pool0, 7)
            dve.tensor_copy(iota_hist[:, :, :], bc_free(iota_i[:, :], HT))
            dve.tensor_copy(iota_w[:, :], iota_i[:, 0:W])
            dve.tensor_copy(window_off[:, :], window_i[:, :])
            dve.memset(count[:, :], 0.0).then_inc(s_iota, 1)

            def from_psum(b):
                return [banks[b + h][:, :].rearrange("p (j s) -> p s j", s=P)[:, 0:NS, :] for h in range(2)]
            dve.wait_ge(s_idxT, 1)
            for h, ps in enumerate(from_psum(0)):
                last = dve.tensor_copy(dst_col[:, :, 4 * h:4 * h + 4], ps)
            last.then_inc(s_dstcol, 1)
            dve.wait_ge(s_dstcol, 1)
            dve.tensor_single_scalar(part_i[:, :, :], dst_col[:, :, :], 7, ALU.arith_shift_right).then_inc(s_split, 1)
            dve.wait_ge(s_split, 1)
            dve.tensor_copy(hi_col[:, :], part_i[:, :, :].rearrange("p s j -> p (s j)")).then_inc(s_split, 1)
            dve.wait_ge(s_split, 2)
            dve.tensor_single_scalar(part_i[:, :, :], dst_col[:, :, :], 127, ALU.bitwise_and).then_inc(s_split, 1)
            dve.wait_ge(s_split, 3)
            dve.tensor_copy(lo_col[:, :], part_i[:, :, :].rearrange("p s j -> p (s j)")).then_inc(s_split, 1)
            dve.wait_ge(s_idxT, 2)
            for h, ps in enumerate(from_psum(2)):
                last = dve.tensor_copy(src_col[:, :, 4 * h:4 * h + 4], ps)
            last.then_inc(s_srccol, 1)

            dve.wait_ge(s_dve0, 2)
            dve.tensor_reduce(base_span[:, 0:1], dst_f[:, :], AX.X, ALU.min).then_inc(s_red, 1)
            dve.scalar_tensor_tensor(src_f[:, :], dst_f[:, :], float(PAD_LIMIT), dst_f[:, :],
                                     ALU.is_lt, ALU.mult).then_inc(s_red, 1)
            dve.wait_ge(s_red, 2)
            dve.tensor_reduce(base_used[:, 0:1], src_f[:, :], AX.X, ALU.max).then_inc(s_red, 1)
            dve.wait_ge(s_red, 3)
            dve.tensor_tensor(base_span[:, 1:2], base_used[:, 0:1], base_span[:, 0:1], ALU.subtract).then_inc(s_span, 1)
            dve.wait_ge(s_base, 1)
            dve.tensor_reduce(span_max[:, :], banks[4][0:1, P:P + NS], AX.X, ALU.max).then_inc(s_small, 1)
            dve.wait_ge(s_small, 1)
            dve.tensor_single_scalar(is_banded[:, :], span_max[:, :], float(W) - 0.5, ALU.is_lt).then_inc(s_flag, 1)
            dve.wait_ge(s_flag, 1)
            dve.tensor_scalar(nwin_f[:, :], is_banded[:, :], float(1 - NW), float(NW), ALU.mult, ALU.add).then_inc(s_small, 1)
            dve.tensor_scalar(base_row_f[:, :], banks[4][0:1, 0:NS], is_banded[0:1, 0:1], None, ALU.mult).then_inc(s_small, 1)
            dve.wait_ge(s_small, 3)
            dve.tensor_copy(nwin_i[:, :], nwin_f[:, :]).then_inc(s_small, 1)
            dve.tensor_copy(base_row[:, :], base_row_f[:, :]).then_inc(s_small, 1)
            dve.wait_ge(s_band, 1)
            dve.tensor_tensor(base_used[:, :], banks[5][0:NS, 0:1], base_span[:, 0:1], ALU.mult).then_inc(s_red, 1)
            dve.wait_ge(s_red, 4)
            dve.tensor_scalar(dst_f[:, :], dst_f[:, :], base_used[:, 0:1], None, ALU.subtract).then_inc(s_rel, 1)
            dve.wait_ge(s_relT, 1)
            for h, ps in enumerate(from_psum(4)):
                last = dve.tensor_copy(rel_col[:, :, 4 * h:4 * h + 4], ps)
            last.then_inc(s_relcol, 1)

            dve.wait_ge(s_x, 32)
            for b in range(NB):
                if b >= 2 * CB:
                    dve.wait_ge(s_bn1, 2 * (b - 2 * CB) + 2)
                dve.bn_stats(stats[:, (b // CB) % 2, b % CB, :], x_sb[:, b, :]).then_inc(s_bn1, 1)
                if b >= 1:
                    dve.wait_ge(s_bn1, 2 * b - 1 if b > 1 else 1)
                    last = dve.bn_aggr(mv[:, b - 1, :], stats[:, ((b - 1) // CB) % 2, (b - 1) % CB, :]).then_inc(s_bn1, 1)
            dve.wait_ge(s_bn1, 2 * NB - 1)
            dve.bn_aggr(mv[:, NB - 1, :], stats[:, ((NB - 1) // CB) % 2, (NB - 1) % CB, :]).then_inc(s_bn1, 1)
            dve.wait_ge(s_bn1, 2 * NB)
            dve.sem_inc(s_bnall, 1)
            dve.wait_ge(s_std, 1)
            dve.reciprocal(rstd[:, :], rstd[:, :]).then_inc(s_small, 1)
            dve.wait_ge(s_small, 6)
            dve.scalar_tensor_tensor(nmr[:, :], mv[:, :, 0], -1.0, rstd[:, :], ALU.mult, ALU.mult).then_inc(s_rstd, 1)

            dve.wait_ge(s_iota, 1)
            dve.wait_ge(s_split, 4)

            def hist(g, h, wait):
                if wait:
                    dve.wait_ge(s_histmm, g - 1)
                dve.tensor_tensor(oh_lo[:, h], lo_col[:, bass.ds(g * HT, HT)].rearrange("p (o t) -> p o t", o=1).to_broadcast([P, P, HT]),
                                  iota_hist[:, :, :], ALU.is_equal)
                dve.tensor_tensor(oh_hi[:, h], hi_col[:, bass.ds(g * HT, HT)].rearrange("p (o t) -> p o t", o=1).to_broadcast([P, HI, HT]),
                                  iota_hist[:, 0:HI, :], ALU.is_equal).then_inc(s_hist, 1)
            hist(0, 0, False)
            hist(1, 1, False)
            with dve.Fori(1, GROUPS // 2) as i:
                hist(2 * i, 0, True)
                hist(2 * i + 1, 1, True)

            dve.wait_ge(s_histmm, GROUPS)
            dve.tensor_copy(count[:, 0:HI], banks[7][:, 0:HI]).then_inc(s_degree, 1)
            dve.wait_ge(s_degree, 1)
            dve.tensor_single_scalar(rcount[:, :], count[:, :], 1.0, ALU.max).then_inc(s_small, 1)
            dve.wait_ge(s_small, 7)
            dve.reciprocal(rcount[:, :], rcount[:, :]).then_inc(s_small, 1)
            dve.wait_ge(s_sdeg, 1)
            dve.reciprocal(dinv[:, :], dinv[:, :]).then_inc(s_small, 1)
            dve.wait_ge(s_small, 9)
            dve.wait_ge(s_u, NCH)

            def scale_rows(c, n, h, m):
                dve.tensor_tensor(blk(node_u, c), blk(node_u, c), bc_free(dinv[:, bass.ds(c * CB, CB)], P),
                                  ALU.mult).then_inc(s_t1, 1)
            chunks(dve, scale_rows)

            def copy_own(c, n, h, m):
                if n >= 2:
                    dve.wait_ge(s_selfT, c - 1)
                dve.tensor_copy(q3(st[:, h]), blk(node_u, c)).then_inc(s_own, 1)
            dve.wait_ge(s_t1, NCH)
            chunks(dve, copy_own)

            def diagonal(c, n, h, m):
                if n >= 2:
                    dve.wait_ge(s_dbc, c - 1)
                dve.tensor_tensor(q3(z[:, h]), bc_mid(ident[:, :], CB), bc_free(dinv[:, bass.ds(c * CB, CB)], P),
                                  ALU.mult).then_inc(s_diag, 1)
            chunks(dve, diagonal)

            def add_b2(c, n, h, m):
                dve.tensor_tensor(blk(x_sb, c), blk(x_sb, c), bc_mid(b2_bc[:, :], CB), ALU.add).then_inc(s_xb, 1)
            chunks(dve, add_b2)

            dve.wait_ge(s_small, 9)
            dve.wait_ge(s_relcol, 1)
            nwin = dve.value_load(nwin_i[0:1, 0:1], min_val=1, max_val=NW)
            done = dve.alloc_register("windows_dve")
            dve.reg_mov(done, 0)

            def sum_supertile(s):
                base = dve.value_load(base_row[0:1, bass.ds(s, 1)], min_val=0, max_val=N - 1)
                with dve.Fori(0, nwin) as k:
                    dve.reg_add(done, done, 1)
                    d = dve.snap(done)
                    dve.scalar_tensor_tensor(oh[:, :, :], rel_col[:, bass.ds(s, 1), :].rearrange("p s (j o) -> p (s j) o", o=1).to_broadcast([P, TILES, W]),
                                             window_off[:, bass.ds(k, 1)], bc_mid(iota_w[:, :], TILES),
                                             ALU.subtract, ALU.is_equal).then_inc(s_oh, 1)
                    start = nc.s_assert_within(base + k * W, 0, NP - W, skip_runtime_bounds_check_because="base is 0 where k is above 0")
                    dve.wait_ge(s_agg, d)
                    dve.tensor_tensor(acc[:, bass.ds(start, W)], acc[:, bass.ds(start, W)], banks[6][:, 0:W],
                                      ALU.add).then_inc(s_added, 1)
                    dve.wait_ge(s_added, d)
                dve.sem_inc(s_free, 1)

            def gcn_phase(ph):
                dve.wait_ge(s_acc0, NCH * (ph + 1))
                with dve.Fori(0, BODIES) as i:
                    for u in range(RING):
                        sum_supertile(RING * i + u)
            gcn_phase(0)

            dve.wait_ge(s_dbcc, NCH)

            def second_z(c, n, h, m):
                if n >= 2:
                    dve.wait_ge(s_zw, c - 1)
                dve.tensor_tensor(z[:, h], cols(acc, c), cols(dinv_bc, c), ALU.mult).then_inc(s_z, 1)
                if n >= 1:
                    second_table(c - 1, n - 1, 1 - h, m - (1 - h))

            def second_table(c, n, h, m):
                dve.wait_ge(s_zw, c + 1)
                if n >= 2:
                    dve.wait_ge(s_tab[h], 16 * m + STORES[h])
                    dve.wait_ge(s_selfT, NCH + c - 1)
                dve.tensor_tensor(q3(st[:, h]), q3(banks[h][:, :]), bc_free(dinv[:, bass.ds(c * CB, CB)], P),
                                  ALU.mult).then_inc(s_t, 1)
            chunks(dve, second_z)
            second_table(NCH - 1, 9, (NCH - 1) % 2, (NCH - 1) // 2)
            gcn_phase(1)

            def third_x2(c, n, h, m):
                dve.wait_ge(s_c["tr"], c + 1)
                dve.tensor_tensor(blk(x_sb, c), q3(banks[h][:, :]), blk(x_sb, c), ALU.add).then_inc(s_c["x2"], 1)
                dve.wait_ge(s_c["x2"], c + 1)
                norms(c, s_c, lambda k: x_sb[:, c * CB + k, :], h)
                if n >= 1:
                    third_rows(c - 1, n - 1, 1 - h, m - (1 - h))

            def norms(c, sems, rows, h):
                next_norm()
                for k in range(CB):
                    dve.bn_stats(stats[:, h, k, :], rows(k)).then_inc(sems["bn"], 1)
                for k in range(CB):
                    dve.wait_ge(sems["bn"], 2 * CB * c + CB + k)
                    next_norm()
                    dve.bn_aggr(cmv[:, h, k, :], stats[:, h, k, :]).then_inc(sems["bn"], 1)

            def scales(c, sems, h):
                dve.wait_ge(sems["std"], c + 1)
                dve.reciprocal(crstd[:, h], cstd[:, h]).then_inc(sems["rstd"], 1)
                dve.wait_ge(sems["rstd"], 2 * c + 1)
                dve.scalar_tensor_tensor(cnmr[:, h], cmv[:, h, :, 0], -1.0, crstd[:, h],
                                         ALU.mult, ALU.mult).then_inc(sems["rstd"], 1)

            def third_rows(c, n, h, m):
                scales(c, s_c, h)
                dve.wait_ge(s_c["hw"], 2 * c + 1)
                if n >= 2:
                    dve.wait_ge(s_tab[h], 16 * m + 2 * STORES[h])
                dve.tensor_tensor(q3(st[:, h]), q3(banks[4][:, :]), bc_mid(bmsg_bc[:, :], CB),
                                  ALU.add).then_inc(s_c["t3"], 1)
            chunks(dve, third_x2)
            third_rows(NCH - 1, 9, (NCH - 1) % 2, (NCH - 1) // 2)

            def add_bupd(c, n, h, m):
                dve.tensor_tensor(blk(node_u, c), blk(node_u, c), bc_mid(bupd_bc[:, :], CB), ALU.add).then_inc(s_ub, 1)
            dve.wait_ge(s_c["u"], NCH)
            chunks(dve, add_bupd)

            dve.wait_ge(s_acc0, NCH * 3)

            def message_body(i, first, last):
                for u in range(RING):
                    dve.wait_ge(s_g[u], 16 * TILES * i + 16 * TILES * (2 * BODIES + 1))
                    for half in range(2):
                        dve.wait_ge(s_m, 2 * RING * i + 2 * u + half + 1)
                        rows = G[:, u, 4 * half:4 * half + 4, :]
                        dve.tensor_tensor(rows, q3(banks[2 + 2 * (u % 2) + half][:, :]), rows, ALU.add).then_inc(s_msum, 1)
                    sum_supertile(RING * i + u)
            bodies(dve, message_body)

            def end_y(c, n, h, m):
                dve.wait_ge(s_d["mm"], c + 1)
                dve.tensor_tensor(q3(hT[:, h]), q3(banks[h][:, :]), bc_free(rcount[:, bass.ds(c * CB, CB)], P),
                                  ALU.mult).then_inc(s_d["y1"], 1)
                dve.wait_ge(s_d["y1"], c + 1)
                dve.tensor_tensor(q3(hT[:, h]), q3(hT[:, h]), blk(node_u, c), ALU.add).then_inc(s_d["y"], 1)
                dve.wait_ge(s_d["y"], c + 1)
                norms(c, s_d, lambda k: hT[:, h, k * P:(k + 1) * P], h)
                scales(c, s_d, h)
                if n >= 1:
                    end_rows(c - 1, n - 1, 1 - h, m - (1 - h))

            def end_rows(c, n, h, m):
                dve.wait_ge(s_d["g"], c + 1)
                dve.tensor_tensor(q3(st[:, h]), q3(st[:, h]), blk(hb_all, c), ALU.add).then_inc(s_d["b"], 1)
                dve.wait_ge(s_d["b"], c + 1)
                if n >= 2:
                    dve.wait_ge(s_out[h], 16 * m)
                dve.scalar_tensor_tensor(y[:, h], st[:, h], 0.0, blk(x_sb, c).rearrange("p k f -> p (k f)"),
                                         ALU.max, ALU.add).then_inc(s_d["fin"], 1)
            dve.wait_ge(s_c["hb"], NCH)
            dve.wait_ge(s_ub, NCH)
            chunks(dve, end_y)
            end_rows(NCH - 1, 9, (NCH - 1) % 2, (NCH - 1) // 2)


_INS = ["x", "src", "dst", "edge_attr_128", "L0_gnn_W1", "L0_gnn_b1", "L0_gnn_W2", "L0_gnn_b2",
        "L1_gnn_W_msg", "L1_gnn_b_msg", "L1_gnn_W_upd", "L1_gnn_b_upd", "L1_gnn_gamma", "L1_gnn_beta"]


def kernel(**inputs):
    import numpy as _np
    import concourse.bacc as _bacc
    from concourse import mybir as _mybir
    from concourse.bass_utils import run_bass_kernel_spmd as _run

    nc = _bacc.Bacc("TRN2", target_bir_lowering=False, num_devices=1)
    arrays, args = {}, []
    for name in _INS:
        a = _np.ascontiguousarray(inputs[name])
        arrays[f"in_{name}"] = a
        args.append(nc.dram_tensor(f"in_{name}", a.shape, _mybir.dt.from_np(a.dtype), kind="ExternalInput").ap())
    shape = inputs["x"].shape
    args.append(nc.dram_tensor("out_x", tuple(shape), _mybir.dt.float32, kind="ExternalOutput").ap())
    gnn_program(nc, *args)
    r = _run(nc, [arrays], core_ids=[0])
    return r.results[0]["out_x"]
```

```python
import concourse.bass as bass
from concourse import mybir
from contextlib import ExitStack

P = 128
TILES = 8
W = 96
RING = 4
CB = 4
CH = CB * P
HT = 16
PAD_DST = 16384
PAD_LIMIT = 8192
EPS = 1e-5


def gnn_program(nc, x, src, dst, edge, W1, b1, W2, b2, W_msg, b_msg, W_upd, b_upd, gamma, beta, out):
    f32, i32, bf16 = mybir.dt.float32, mybir.dt.int32, mybir.dt.bfloat16
    ALU, ACT, AX = mybir.AluOpType, mybir.ActivationFunctionType, mybir.AxisListType

    N = x.shape[0]
    E = src.shape[0]
    SE = P * TILES
    NS = -(-E // (SE * RING)) * RING
    FULL = E // SE
    LAST = E - FULL * SE
    assert NS == FULL + 1 and LAST > 0 and NS <= P
    BODIES = NS // RING
    NCH = -(-N // CH)
    NB = NCH * CB
    NP = NB * P
    assert NCH % 2 == 1 and NCH >= 5
    XB = N // P
    XR = N - XB * P
    HI = -(-N // P)
    NW = -(-N // W)
    assert NW * W <= NP and N - 1 + W <= NP and N < PAD_LIMIT
    GROUPS = NS * TILES // HT
    assert GROUPS % 2 == 0 and GROUPS >= 6

    table = nc.dram_tensor("table", (NP, P), f32, kind="Internal").ap()

    ctx = ExitStack()
    with ctx:
        def sb(name, shape, dt=f32):
            return ctx.enter_context(nc.sbuf_tensor(name, shape, dt))

        def sem(name):
            return ctx.enter_context(nc.semaphore(name))

        w1 = sb("w1", [P, P])
        w2 = sb("w2", [P, P])
        w_node = sb("w_node", [P, 2 * P])
        w_edge = sb("w_edge", [P, P])
        w_mean = sb("w_mean", [P, P])
        b1_col = sb("b1_col", [P, 1])
        b2_bc = sb("b2_bc", [P, P])
        bmsg_bc = sb("bmsg_bc", [P, P])
        bupd_col = sb("bupd_col", [P, 1])
        gamma_bc = sb("gamma_bc", [P, P])
        beta_bc = sb("beta_bc", [P, P])
        ident = sb("ident", [P, P])
        ones = sb("ones", [P, P])
        zeros = sb("zeros", [P, CH])
        iota_i = sb("iota_i", [P, P], i32)
        iota_w = sb("iota_w", [P, W])
        window_i = sb("window_i", [P, NW], i32)
        window_off = sb("window_off", [P, NW])
        eps_col = sb("eps_col", [P, 1])

        src_col = sb("src_col", [P, NS, TILES], i32)
        rel_col = sb("rel_col", [P, NS, TILES])
        base_span = sb("base_span", [NS, 2])
        base_row_f = sb("base_row_f", [1, NS])
        base_row = sb("base_row", [1, NS], i32)
        span_max = sb("span_max", [1, 1])
        is_banded = sb("is_banded", [1, 1])
        nwin_f = sb("nwin_f", [1, 1])
        nwin_i = sb("nwin_i", [1, 1], i32)
        banded_col = sb("banded_col", [NS, 1])
        base_used = sb("base_used", [NS, 1])

        x_sb = sb("x_sb", [P, NB, P])
        acc = sb("acc", [P, NP])
        dinv_bc = sb("dinv_bc", [P, NP])
        rc_bc = sb("rc_bc", [P, NP])
        node_u = sb("node_u", [P, NB, P])
        hT_all = node_u[:, :, :].rearrange("p b f -> p (b f)")
        hb_all = dinv_bc[:, :].rearrange("p (b f) -> p b f", f=P)
        count = sb("count", [P, NB])
        dinv = sb("dinv", [P, NB])
        rcount = sb("rcount", [P, NB])
        neg_mean = sb("neg_mean", [P, NB])
        sq_sum = sb("sq_sum", [P, NB])
        rstd = sb("rstd", [P, NB])
        nmr = sb("nmr", [P, NB])

        acc_bf = acc[:, :].bitcast(bf16)
        iota_hist = acc_bf[:, 0:P * HT].rearrange("p (v t) -> p v t", t=HT)
        oh_lo = acc_bf[:, P * HT:3 * P * HT].rearrange("p (h v t) -> p h v t", h=2, t=HT)
        oh_hi = acc_bf[:, 3 * P * HT:(3 * P + 2 * HI) * HT].rearrange("p (h v t) -> p h v t", h=2, t=HT)
        C = NS * TILES
        assert 4 * C <= NP
        dst_col, hi_i, lo_i = [dinv_bc[:, n * C:(n + 1) * C].bitcast(i32) for n in range(3)]
        hilo = dinv_bc[:, 3 * C:4 * C].bitcast(bf16)
        hi_col, lo_col = hilo[:, 0:C], hilo[:, C:2 * C]

        G = sb("G", [P, RING, TILES, P])
        edges = sb("edges", [P, RING, TILES, P])
        dst_rows, src_rows, dst_f, src_f = [edges[0:NS, u].rearrange("s j f -> s (j f)") for u in range(4)]
        dst_rows, src_rows = dst_rows.bitcast(i32), src_rows.bitcast(i32)
        idx_ring = sb("idx_ring", [P, RING, TILES], i32)
        edgeT = sb("edgeT", [P, 2, CH])
        oh = sb("oh", [P, TILES, W])
        z = sb("z", [P, 2, CH])
        st = sb("st", [P, 2, CH])
        hT = sb("hT", [P, 2, CH])
        y = sb("y", [P, 2, CH])
        stats = sb("stats", [P, 2, CB, 6])
        cmv = sb("cmv", [P, 2, CB, 2])
        cstd = sb("cstd", [P, 2, CB])
        crstd = sb("crstd", [P, 2, CB])
        cnmr = sb("cnmr", [P, 2, CB])

        banks = [ctx.enter_context(nc.psum_tensor(f"bank{i}", [P, 512], f32)) for i in range(8)]

        s_loads = sem("s_loads")
        s_x = sem("s_x")
        s_idx = [sem("s_idx_dst"), sem("s_idx_src")]
        s_pool0 = sem("s_pool0")
        s_dve0 = sem("s_dve0")
        s_pad = sem("s_pad")
        s_idxT = sem("s_idxT")
        s_base = sem("s_base")
        s_band = sem("s_band")
        s_relT = sem("s_relT")
        s_hist = sem("s_hist")
        s_histmm = sem("s_histmm")
        s_std = sem("s_std")
        s_rstd = sem("s_rstd")
        s_sdeg = sem("s_sdeg")
        s_h = sem("s_h")
        s_hTp = sem("s_hTp")
        s_hTc = sem("s_hTc")
        s_hw = sem("s_hw")
        s_u = sem("s_u")
        s_t1 = sem("s_t1")
        s_tab = [sem(f"s_tab{h}") for h in range(2)]
        s_selfT = sem("s_selfT")
        s_acc0 = sem("s_acc0")
        s_diag = sem("s_diag")
        s_dbc = sem("s_dbc")
        s_dbcc = sem("s_dbcc")
        s_xb = sem("s_xb")
        s_idxr = sem("s_idxr")
        s_g = [sem(f"s_g{u}") for u in range(RING)]
        s_free = sem("s_free")
        s_oh = sem("s_oh")
        s_agg = sem("s_agg")
        s_added = sem("s_added")
        s_z = sem("s_z")
        s_zr = sem("s_zr")
        s_zw = sem("s_zw")
        s_t = sem("s_t")
        s_c = {n: sem("s_c_" + n) for n in
               ("z", "tr", "zero", "x2", "bn", "std", "rstd", "h", "hT", "hTc", "hTa", "hw", "t3", "hb")}
        s_started_pool = sem("s_started_pool")
        s_started_pe = sem("s_started_pe")
        s_started_dve = sem("s_started_dve")
        s_mean = sem("s_mean")
        s_sq = sem("s_sq")
        s_srcf = sem("s_srcf")
        s_hilo = sem("s_hilo")
        s_zero = sem("s_zero")
        s_degree = sem("s_degree")
        s_srccol = sem("s_srccol")
        s_dstcol = sem("s_dstcol")
        s_split = sem("s_split")
        s_iota = sem("s_iota")
        s_red = sem("s_red")
        s_span = sem("s_span")
        s_small = sem("s_small")
        s_flag = sem("s_flag")
        s_rel = sem("s_rel")
        s_relcol = sem("s_relcol")
        s_own = sem("s_own")
        s_e = [sem(f"s_e{u}") for u in range(RING)]
        s_eT = sem("s_eT")
        s_eTc = sem("s_eTc")
        s_m = sem("s_m")
        s_msum = sem("s_msum")
        s_msg = sem("s_msg")
        s_d = {n: sem("s_d_" + n) for n in
               ("z", "mm", "u", "tr", "bn", "std", "rstd", "n", "g", "b", "fin")}
        s_out = [sem(f"s_out{h}") for h in range(2)]

        block = ctx.enter_context(nc.Block())

        def bc_free(ap, n):
            return ap.rearrange("p (k o) -> p k o", o=1).to_broadcast([ap.shape[0], ap.shape[1], n])

        def bc_mid(ap, k):
            return ap.rearrange("p (o n) -> p o n", o=1).to_broadcast([ap.shape[0], k, ap.shape[1]])

        def cols(ap, c):
            return ap[:, bass.ds(c * CH, CH)]

        def blk(ap, c):
            return ap[:, bass.ds(c * CB, CB)]

        def q3(ap):
            return ap.rearrange("p (k f) -> p k f", f=P)

        def pipeline(eng, *steps):
            lags = [lag for lag, _ in steps]

            def turn(t):
                for lag, step in steps:
                    c = t - lag
                    if 0 <= c < NCH:
                        step(c, c, c % 2, c // 2)
            first = max(lags) + 2
            pairs = max(0, (NCH - first) // 2)
            if pairs < 2:
                pairs = 0
            for t in range(first if pairs else NCH + max(lags)):
                turn(t)
            if pairs:
                with eng.Fori(1, pairs + 1) as i:
                    for b in range(2):
                        for lag, step in steps:
                            at = first - 2 + b - lag
                            step(2 * i + at, 2, at % 2, i + at // 2)
                for t in range(first + 2 * pairs, NCH + max(lags)):
                    turn(t)

        def chunks(eng, step):
            pipeline(eng, (0, step))

        def bodies(eng, step):
            step(0, True, False)
            with eng.Fori(1, BODIES - 1) as i:
                step(i, False, False)
            step(BODIES - 1, False, True)

        def counter(eng, started):
            return lambda: eng.sem_inc(started, 1)

        def table_chunk(c):
            return table[bass.ds(c * CH, CH), :].rearrange("(k p) f -> p k f", p=P)

        STORES = [16 * (NCH - NCH // 2), 16 * (NCH // 2)]
        LEAD = GROUPS // 2 - 1 - NCH
        assert LEAD >= 2
        N_WEIGHTS = 6
        N_BIASES = 6

        def from_psum(b):
            return [banks[b + h][:, :].rearrange("p (j s) -> p s j", s=P)[:, 0:NS, :] for h in range(2)]

        @block.sync
        def _(sp):
            sp.wait_ge(s_pad, 1)
            rows = FULL * SE
            sp.dma_start(dst_rows[0:FULL, :], dst[0:rows].rearrange("(s e) -> s e", e=SE)).then_inc(s_idx[0], 16)
            sp.dma_start(dst_rows[FULL:NS, SE - LAST:SE], dst[rows:E].rearrange("(s e) -> s e", s=1)).then_inc(s_idx[0], 16)
            sp.dma_start(src_rows[0:FULL, :], src[0:rows].rearrange("(s e) -> s e", e=SE)).then_inc(s_idx[1], 16)
            sp.dma_start(src_rows[FULL:NS, :], src[E - SE:E].rearrange("(s e) -> s e", s=1)).then_inc(s_idx[1], 16)
            sp.wait_ge(s_pad, 2)
            sp.dma_start(x_sb[:, 0:XB, :], x[0:XB * P, :].rearrange("(b p) f -> p b f", p=P)).then_inc(s_x, 16)
            sp.dma_start(x_sb[0:XR, XB, :], x[XB * P:N, :]).then_inc(s_x, 16)

            def load_edges(i, u, row, wait):
                if wait:
                    sp.wait_ge(s_eT, 2 * RING * i - 2 * RING + 2 * u + 2)
                sp.dma_start(edges[:, u, :, :].rearrange("p j f -> p (j f)"),
                             edge[row, :].rearrange("(p j) f -> p (j f)", p=P)).then_inc(s_e[u], 16)

            def store_scaled(c, n, h, m):
                sp.wait_ge(s_t1, c + 1)
                sp.dma_start(table_chunk(c), blk(node_u, c)).then_inc(s_tab[h], 16)
            chunks(sp, store_scaled)

            sp.wait_ge(s_relT, 1)
            sp.wait_ge(s_red, 4)
            for u in range(RING):
                load_edges(0, u, slice(u * SE, (u + 1) * SE), False)

            def store_second(c, n, h, m):
                sp.wait_ge(s_t, c + 1)
                sp.dma_start(table_chunk(c), q3(st[:, h])).then_inc(s_tab[h], 16)
            chunks(sp, store_second)

            def store_third(c, n, h, m):
                sp.wait_ge(s_c["t3"], c + 1)
                sp.dma_start(table_chunk(c), q3(st[:, h])).then_inc(s_tab[h], 16)
            chunks(sp, store_third)

            with sp.Fori(1, BODIES - 1) as i:
                for u in range(RING):
                    load_edges(i, u, bass.ds(i * (RING * SE) + u * SE, SE), True)
            i = BODIES - 1
            for u in range(RING):
                s = i * RING + u
                row = min(s * SE, E - SE)
                load_edges(i, u, slice(row, row + SE), True)

            def store_out(c, n, h, m):
                sp.wait_ge(s_d["fin"], c + 1)
                sp.dma_start(out[bass.ds(c * CH, CH), :].rearrange("(k p) f -> p k f", p=P),
                             q3(y[:, h])).then_inc(s_out[h], 16)
            for c in range(3):
                store_out(c, c, c % 2, 0)
            whole = N // CH
            pairs = (whole - 3) // 2
            with sp.Fori(1, pairs + 1) as i:
                store_out(2 * i + 1, 3, 1, i)
                store_out(2 * i + 2, 4, 0, i)
            for c in range(3 + 2 * pairs, whole):
                store_out(c, c, c % 2, 0)
            stores = [whole - whole // 2, whole // 2]
            if N > whole * CH:
                sp.wait_ge(s_d["fin"], whole + 1)
                tail = q3(y[:, whole % 2])
                for b in range(whole * CB, HI):
                    n = min(P, N - b * P)
                    sp.dma_start(out[b * P:b * P + n, :], tail[0:n, b - whole * CB, :]).then_inc(s_out[whole % 2], 16)
                    stores[whole % 2] += 1
            for h in range(2):
                sp.wait_ge(s_out[h], 16 * stores[h])

        @block.gpsimd
        def _(pool):
            pool.memset(dst_rows[:, :], PAD_DST).then_inc(s_pad, 1)
            pool.memset(x_sb[:, XB:NB, :], 0.0).then_inc(s_pad, 1)
            pool.memset(ident[:, :], 0.0).then_inc(s_pool0, 1)
            pool.wait_ge(s_pool0, 1)
            pool.affine_select(out=ident[:, :], in_=ident[:, :], compare_op=ALU.not_equal, fill=1.0,
                               base=0, pattern=[[-1, P]], channel_multiplier=1).then_inc(s_pool0, 1)
            pool.iota(iota_i[:, :], pattern=[[1, P]], base=0, channel_multiplier=0).then_inc(s_pool0, 1)
            pool.iota(window_i[:, :], pattern=[[W, NW]], base=0, channel_multiplier=0).then_inc(s_pool0, 1)
            pool.memset(ones[:, :], 1.0).then_inc(s_pool0, 1)
            pool.memset(zeros[:, :], 0.0).then_inc(s_pool0, 1)
            pool.memset(eps_col[:, :], EPS).then_inc(s_pool0, 1)

            next_supertile = counter(pool, s_started_pool)

            def gather_phase(ph):
                def body(i, first, last):
                    for u in range(RING):
                        if not (ph == 0 and first):
                            pool.wait_ge(s_free, RING * i + (ph * NS + u - RING + 1))
                        pool.wait_ge(s_idxr, RING * i + (ph * NS + u + 1))
                        for h in range(2):
                            pool.wait_ge(s_tab[h], STORES[h] * (ph + 1))
                        next_supertile()
                        for j in range(TILES):
                            pool.indirect_dma_start(
                                out=G[:, u, j, :], out_offset=None, in_=table,
                                in_offset=bass.IndirectOffsetOnAxis(ap=idx_ring[:, u, j:j + 1], axis=0),
                            ).then_inc(s_g[u], 16)
                bodies(pool, body)

            gather_phase(0)
            gather_phase(1)

            def third_z(c, n, h, m):
                if n >= 2:
                    pool.wait_ge(s_c["tr"], c - 1)
                pool.tensor_tensor(z[:, h], cols(acc, c), cols(dinv_bc, c), ALU.mult).then_inc(s_c["z"], 1)

            def keep_h(c, n, h, m):
                pool.wait_ge(s_c["h"], c + 1)
                pool.wait_ge(s_c["z"], c + 1)
                pool.tensor_tensor(blk(hb_all, c), q3(y[:, h]), bc_mid(beta_bc[:, :], CB),
                                   ALU.add).then_inc(s_c["hb"], 1)
            pool.wait_ge(s_free, 2 * NS)
            pool.wait_ge(s_loads, 16 * (N_WEIGHTS + N_BIASES))
            pipeline(pool, (0, third_z), (3, keep_h))

            gather_phase(2)

            def end_z(c, n, h, m):
                if n >= 2:
                    pool.wait_ge(s_d["mm"], c - 1)
                pool.tensor_tensor(z[:, h], cols(acc, c), cols(rc_bc, c), ALU.mult).then_inc(s_d["z"], 1)

            def times_gamma(c, n, h, m):
                pool.wait_ge(s_d["n"], c + 1)
                pool.tensor_tensor(q3(st[:, h]), q3(st[:, h]), bc_mid(gamma_bc[:, :], CB),
                                   ALU.mult).then_inc(s_d["g"], 1)
            pool.wait_ge(s_free, 3 * NS)
            pool.wait_ge(s_dbcc, 2 * NCH)
            pipeline(pool, (0, end_z), (5, times_gamma))

        @block.scalar
        def _(act):
            for dram, tile in ((W1, w1[:, :]), (W2, w2[:, :]),
                               (W_msg[0:P, :], w_node[:, 0:P]), (W_upd[0:P, :], w_node[:, P:2 * P]),
                               (W_msg[P:2 * P, :], w_edge[:, :]), (W_upd[P:2 * P, :], w_mean[:, :])):
                act.dma_start(tile, dram).then_inc(s_loads, 16)
            for dram, tile in ((b1, b1_col), (b_upd, bupd_col)):
                act.dma_start(tile[:, :], dram.rearrange("(p o) -> p o", o=1)).then_inc(s_loads, 16)
            for dram, tile in ((b2, b2_bc), (b_msg, bmsg_bc), (gamma, gamma_bc), (beta, beta_bc)):
                act.dma_start(tile[:, :], dram.rearrange("(o f) -> o f", o=1).to_broadcast([P, P])).then_inc(s_loads, 16)

            act.wait_ge(s_idx[1], 32)
            act.activation(src_f, src_rows, ACT.Copy).then_inc(s_srcf, 1)
            act.wait_ge(s_split, 1)
            act.activation(hi_col, hi_i, ACT.Copy).then_inc(s_hilo, 1)
            act.wait_ge(s_split, 2)
            act.activation(lo_col, lo_i, ACT.Copy).then_inc(s_hilo, 1)
            act.wait_ge(s_idxT, 2)
            for b, ps in enumerate(from_psum(2)):
                last = act.activation(src_col[:, :, 4 * b:4 * b + 4], ps, ACT.Copy)
            last.then_inc(s_srccol, 1)

            act.wait_ge(s_pool0, 7)
            act.wait_ge(s_x, 32)

            def first_mean(c, n, h, m):
                for k in range(CB):
                    last = act.activation(node_u[:, bass.ds(c * CB + k, 1), :], x_sb[:, bass.ds(c * CB + k, 1), :],
                                          ACT.Copy, scale=-1.0 / P,
                                          accum_out=neg_mean[:, bass.ds(c * CB + k, 1)])
                last.then_inc(s_mean, 1)

            def first_squares(c, n, h, m):
                act.wait_ge(s_mean, c + 1)
                for k in range(CB):
                    last = act.activation(rc_bc[:, bass.ds((c * CB + k) * P, P)], x_sb[:, c * CB + k, :], ACT.Square,
                                          bias=neg_mean[:, bass.ds(c * CB + k, 1)],
                                          accum_out=sq_sum[:, bass.ds(c * CB + k, 1)])
                last.then_inc(s_sq, 1)
            pipeline(act, (0, first_mean), (1, first_squares))
            act.wait_ge(s_sq, NCH)
            act.activation(rstd[:, :], sq_sum[:, :], ACT.Sqrt, scale=1.0 / P, bias=eps_col[:, 0:1]).then_inc(s_std, 1)
            act.wait_ge(s_rstd, 2)

            def first_h(c, n, h, m):
                if n >= 2:
                    act.wait_ge(s_hTp, c - 1)
                for k in range(CB):
                    last = act.activation(z[:, h, k * P:(k + 1) * P], x_sb[:, c * CB + k, :], ACT.Relu,
                                          scale=rstd[:, bass.ds(c * CB + k, 1)], bias=nmr[:, bass.ds(c * CB + k, 1)])
                last.then_inc(s_h, 1)

            def first_hT(c, n, h, m):
                act.wait_ge(s_hTp, c + 1)
                if n >= 2:
                    act.wait_ge(s_hw, c - 1)
                act.activation(hT[:, h], banks[h][:, :], ACT.Copy).then_inc(s_hTc, 1)

            def first_hw(c, n, h, m):
                act.wait_ge(s_hw, c + 1)
                act.activation(blk(node_u, c), q3(banks[2 + h][:, :]), ACT.Copy).then_inc(s_u, 1)
            pipeline(act, (0, first_h), (1, first_hT), (2, first_hw))

            act.wait_ge(s_degree, 1)
            act.activation(dinv[:, :], count[:, :], ACT.Sqrt, bias=ones[:, 0:1]).then_inc(s_sdeg, 1)

            def fill_indices(ph, i, u, first):
                if not (ph == 0 and first):
                    act.wait_ge(s_g[u], 16 * TILES * i + 16 * TILES * BODIES * ph)
                act.activation(idx_ring[:, u, :], src_col[:, RING * i + u, :], ACT.Copy).then_inc(s_idxr, 1)

            act.wait_ge(s_srccol, 1)
            for u in range(RING):
                fill_indices(0, 0, u, True)

            def copy_own(c, n, h, m):
                act.wait_ge(s_t1, c + 1)
                if n >= 2:
                    act.wait_ge(s_selfT, c - 1)
                act.activation(q3(st[:, h]), blk(node_u, c), ACT.Copy).then_inc(s_own, 1)

            def own_rows(c, n, h, m):
                act.wait_ge(s_selfT, c + 1)
                act.activation(cols(acc, c), banks[h][:, :], ACT.Copy).then_inc(s_acc0, 1)
            pipeline(act, (0, copy_own), (2, own_rows))

            def broadcasts(ph, rows):
                def broadcast_rows(c, n, h, m):
                    act.wait_ge(s_dbc, ph * NCH + c + 1)
                    act.activation(cols(rows, c), banks[2 + h][:, :], ACT.Copy).then_inc(s_dbcc, 1)
                chunks(act, broadcast_rows)
            broadcasts(0, dinv_bc)

            def gcn_phase(ph):
                if ph:
                    for u in range(RING):
                        fill_indices(ph, 0, u, True)
                    broadcasts(1, rc_bc)

                def body(i, first, last):
                    for u in range(RING):
                        if not last:
                            fill_indices(ph, i + 1, u, False)
                bodies(act, body)
            gcn_phase(0)

            def second_z(c, n, h, m):
                act.wait_ge(s_z, c + 1)
                act.activation(z[:, h], z[:, h], ACT.Relu, bias=b1_col[:, 0:1]).then_inc(s_zr, 1)

            def second_own(c, n, h, m):
                act.wait_ge(s_selfT, NCH + c + 1)
                act.activation(cols(acc, c), banks[2 + h][:, :], ACT.Copy).then_inc(s_acc0, 1)
            pipeline(act, (0, second_z), (3, second_own))
            gcn_phase(1)

            def third_std(c, n, h, m):
                act.wait_ge(s_c["bn"], 2 * CB * c + 2 * CB)
                act.activation(cstd[:, h], cmv[:, h, :, 1], ACT.Sqrt, bias=eps_col[:, 0:1]).then_inc(s_c["std"], 1)

            def third_h(c, n, h, m):
                act.wait_ge(s_c["rstd"], 2 * c + 2)
                if n >= 2:
                    act.wait_ge(s_c["hT"], c - 1)
                    act.wait_ge(s_c["hb"], c - 1)
                for k in range(CB):
                    last = act.activation(y[:, h, k * P:(k + 1) * P], x_sb[:, c * CB + k, :], ACT.Relu,
                                          scale=crstd[:, h, k:k + 1], bias=cnmr[:, h, k:k + 1])
                last.then_inc(s_c["h"], 1)

            def third_hT(c, n, h, m):
                act.wait_ge(s_c["hT"], c + 1)
                if n >= 2:
                    act.wait_ge(s_c["hw"], c - 1)
                act.activation(hT[:, h], banks[2 + h][:, :], ACT.Copy).then_inc(s_c["hTc"], 1)
                act.activation(cols(hT_all, c), banks[2 + h][:, :], ACT.Copy).then_inc(s_c["hTa"], 1)
            pipeline(act, (2, third_h), (3, third_hT), (0, third_std))

            def copy_edges(i, u, first):
                for half in range(2):
                    n = 2 * RING * i + 2 * u + half
                    act.wait_ge(s_eT, n + 1)
                    if not first:
                        act.wait_ge(s_m, n - 1)
                    act.activation(edgeT[:, half], banks[half][:, :], ACT.Copy).then_inc(s_eTc, 1)

            for u in range(RING):
                fill_indices(2, 0, u, True)
            copy_edges(0, 0, True)

            def message_body(i, first, last):
                for u in range(RING):
                    if not (last and u == RING - 1):
                        copy_edges(i if u < RING - 1 else i + 1, (u + 1) % RING, False)
                    for half in range(2):
                        act.wait_ge(s_msum, 2 * RING * i + 2 * u + half + 1)
                        act.activation(G[:, u, 4 * half:4 * half + 4, :], G[:, u, 4 * half:4 * half + 4, :],
                                       ACT.Relu).then_inc(s_msg, 1)
                    if not last:
                        fill_indices(2, i + 1, u, False)
            bodies(act, message_body)

            def end_update(c, n, h, m):
                act.wait_ge(s_d["mm"], c + 1)
                if n >= 2:
                    act.wait_ge(s_d["tr"], c - 1)
                act.activation(hT[:, h], banks[h][:, :], ACT.Identity, bias=bupd_col[:, 0:1]).then_inc(s_d["u"], 1)

            def end_std(c, n, h, m):
                act.wait_ge(s_d["bn"], 2 * CB * c + 2 * CB)
                act.activation(cstd[:, h], cmv[:, h, :, 1], ACT.Sqrt, bias=eps_col[:, 0:1]).then_inc(s_d["std"], 1)

            def end_norm(c, n, h, m):
                act.wait_ge(s_d["rstd"], 2 * c + 2)
                if n >= 2:
                    act.wait_ge(s_d["b"], c - 1)
                for k in range(CB):
                    last = act.activation(st[:, h, k * P:(k + 1) * P], banks[2 + h][:, k * P:(k + 1) * P], ACT.Identity,
                                          scale=crstd[:, h, k:k + 1], bias=cnmr[:, h, k:k + 1])
                last.then_inc(s_d["n"], 1)
            pipeline(act, (4, end_norm), (1, end_update), (3, end_std))

        @block.tensor
        def _(pe):
            pe.wait_ge(s_pool0, 7)
            pe.wait_ge(s_dve0, 1)
            for j in range(TILES):
                last = pe.transpose(banks[j // 4][:, (j % 4) * P:(j % 4) * P + NS],
                                    dst_f[:, :].rearrange("s (p j) -> s p j", j=TILES)[:, :, j],
                                    ident[0:NS, 0:NS])
            last.then_inc(s_idxT, 1)
            pe.wait_ge(s_srcf, 1)
            for j in range(TILES):
                last = pe.transpose(banks[2 + j // 4][:, (j % 4) * P:(j % 4) * P + NS],
                                    src_f[:, :].rearrange("s (p j) -> s p j", j=TILES)[:, :, j],
                                    ident[0:NS, 0:NS])
            last.then_inc(s_idxT, 1)

            def hist(g, h, start, stop):
                pe.wait_ge(s_hist, g + 1)
                for t in range(HT):
                    last = pe.matmul(banks[7][:, 0:HI], oh_lo[:, h, :, t], oh_hi[:, h, :, t],
                                     start=start and t == 0, stop=stop and t == HT - 1)
                last.then_inc(s_histmm, 1)

            def first_tr(c, n, h, m):
                pe.wait_ge(s_h, c + 1)
                if n >= 2:
                    pe.wait_ge(s_hTc, c - 1)
                for k in range(CB):
                    last = pe.transpose(banks[h][:, k * P:(k + 1) * P], z[:, h, k * P:(k + 1) * P], ident[:, :])
                last.then_inc(s_hTp, 1)

            def first_mm(c, n, h, m):
                pe.wait_ge(s_hTc, c + 1)
                if n >= 2:
                    pe.wait_ge(s_u, c - 1)
                for k in range(CB):
                    last = pe.matmul(banks[2 + h][:, k * P:(k + 1) * P], hT[:, h, k * P:(k + 1) * P], w1[:, :],
                                     start=True, stop=True)
                last.then_inc(s_hw, 1)

            pe.wait_ge(s_loads, 16 * (N_WEIGHTS + N_BIASES))
            pe.wait_ge(s_dstcol, 1)
            pe.wait_ge(s_srccol, 1)
            hist(0, 0, True, False)
            hist(1, 1, False, False)
            with pe.Fori(1, LEAD) as i:
                hist(2 * i, 0, False, False)
                hist(2 * i + 1, 1, False, False)

            def beside(c, n, h, m):
                hist(2 * c + 2 * LEAD, 0, False, False)
                hist(2 * c + 2 * LEAD + 1, 1, False, False)
                first_tr(c, n, h, m)
            pipeline(pe, (0, beside), (1, first_mm))
            hist(GROUPS - 2, 0, False, False)
            hist(GROUPS - 1, 1, False, True)

            def own_rows(c, n, h, m):
                pe.wait_ge(s_own, c + 1)
                if n == 0:
                    pe.wait_ge(s_u, NCH)
                if n >= 2:
                    pe.wait_ge(s_acc0, c - 1)
                for k in range(CB):
                    last = pe.transpose(banks[h][:, k * P:(k + 1) * P], st[:, h, k * P:(k + 1) * P], ident[:, :])
                last.then_inc(s_selfT, 1)
            chunks(pe, own_rows)

            pe.wait_ge(s_span, 1)
            pe.transpose(banks[4][0:1, 0:NS], base_span[:, 0:1], ident[0:NS, 0:NS])
            pe.transpose(banks[4][0:1, P:P + NS], base_span[:, 1:2], ident[0:NS, 0:NS]).then_inc(s_base, 1)
            pe.wait_ge(s_flag, 1)
            pe.matmul(banks[5][0:NS, 0:1], ones[0:1, 0:NS], is_banded[0:1, 0:1], start=True, stop=True).then_inc(s_band, 1)
            pe.wait_ge(s_rel, 1)
            for j in range(TILES):
                last = pe.transpose(banks[4 + j // 4][:, (j % 4) * P:(j % 4) * P + NS],
                                    dst_f[:, :].rearrange("s (p j) -> s p j", j=TILES)[:, :, j],
                                    ident[0:NS, 0:NS])
            last.then_inc(s_relT, 1)

            def broadcasts(ph):
                def broadcast_rows(c, n, h, m):
                    pe.wait_ge(s_diag, ph * NCH + c + 1)
                    if ph or n >= 2:
                        pe.wait_ge(s_dbcc, ph * NCH + (c - 1 if n >= 2 else 0))
                    pe.matmul(banks[2 + h][:, :], ones[:, :], z[:, h], start=True, stop=True).then_inc(s_dbc, 1)
                chunks(pe, broadcast_rows)
            broadcasts(0)

            nwin = pe.value_load(nwin_i[0:1, 0:1], min_val=1, max_val=NW)
            next_supertile = counter(pe, s_started_pe)
            done = pe.alloc_register("windows_pe")
            pe.reg_mov(done, 0)

            def sum_supertile(u):
                next_supertile()
                with pe.Fori(0, nwin):
                    pe.reg_add(done, done, 1)
                    d = pe.snap(done)
                    pe.wait_ge(s_oh, d)
                    for j in range(TILES):
                        last = pe.matmul(banks[6][:, 0:W], G[:, u, j, :], oh[:, j, :], start=j == 0, stop=j == TILES - 1)
                    last.then_inc(s_agg, 1)

            def gcn_phase(ph):
                with pe.Fori(0, BODIES) as i:
                    for u in range(RING):
                        pe.wait_ge(s_g[u], 16 * TILES * i + 16 * TILES * (BODIES * ph + 1))
                        sum_supertile(u)
            gcn_phase(0)

            def second_mm(c, n, h, m):
                pe.wait_ge(s_zr, c + 1)
                if n >= 2:
                    pe.wait_ge(s_t, c - 1)
                for k in range(CB):
                    last = pe.matmul(banks[h][:, k * P:(k + 1) * P], z[:, h, k * P:(k + 1) * P], w2[:, :],
                                     start=True, stop=True)
                last.then_inc(s_zw, 1)

            def second_own(c, n, h, m):
                pe.wait_ge(s_t, c + 1)
                if n >= 2:
                    pe.wait_ge(s_acc0, NCH + c - 1)
                for k in range(CB):
                    last = pe.transpose(banks[2 + h][:, k * P:(k + 1) * P], st[:, h, k * P:(k + 1) * P], ident[:, :])
                last.then_inc(s_selfT, 1)
            pipeline(pe, (0, second_mm), (2, second_own))
            pe.wait_ge(s_acc0, 2 * NCH)
            broadcasts(1)
            gcn_phase(1)

            def third_tr(c, n, h, m):
                pe.wait_ge(s_c["z"], c + 1)
                if n >= 2:
                    pe.wait_ge(s_c["x2"], c - 1)
                for k in range(CB):
                    last = pe.transpose(banks[h][:, k * P:(k + 1) * P], z[:, h, k * P:(k + 1) * P], ident[:, :])
                last.then_inc(s_c["tr"], 1)

            def third_hT(c, n, h, m):
                pe.wait_ge(s_c["h"], c + 1)
                if n >= 2:
                    pe.wait_ge(s_c["hTa"], c - 1)
                for k in range(CB):
                    last = pe.transpose(banks[2 + h][:, k * P:(k + 1) * P], y[:, h, k * P:(k + 1) * P], ident[:, :])
                last.then_inc(s_c["hT"], 1)

            def third_mm(c, n, h, m):
                pe.wait_ge(s_c["hTc"], c + 1)
                if n >= 2:
                    pe.wait_ge(s_c["t3"], c - 1)
                for k in range(CB):
                    last = pe.matmul(banks[4 + h][:, k * P:(k + 1) * P], hT[:, h, k * P:(k + 1) * P],
                                     w_node[:, 0:P], start=True, stop=True)
                last.then_inc(s_c["hw"], 1)
            pipeline(pe, (0, third_tr), (3, third_hT), (4, third_mm))

            def transpose_edges(i, u, n):
                pe.wait_ge(s_e[u], 16 * i + 16)
                for half in range(2):
                    if n >= 1:
                        pe.wait_ge(s_eTc, 2 * RING * i + 2 * u + half - 1)
                    for k in range(4):
                        last = pe.transpose(banks[half][:, k * P:(k + 1) * P], edges[:, u, 4 * half + k, :], ident[:, :])
                    last.then_inc(s_eT, 1)

            def edge_products(i, u, n):
                for half in range(2):
                    m = 2 * RING * i + 2 * u + half
                    pe.wait_ge(s_eTc, m + 1)
                    if n >= 2:
                        pe.wait_ge(s_msum, m - 3)
                    for k in range(4):
                        last = pe.matmul(banks[2 + 2 * (u % 2) + half][:, k * P:(k + 1) * P],
                                         edgeT[:, half, k * P:(k + 1) * P], w_edge[:, :], start=True, stop=True)
                    last.then_inc(s_m, 1)

            pe.wait_ge(s_c["t3"], NCH)
            pe.wait_ge(s_c["hTa"], NCH)
            transpose_edges(0, 0, 0)
            edge_products(0, 0, 0)

            def message_body(i, first, last):
                for u in range(RING):
                    if not (last and u == RING - 1):
                        nxt = (i if u < RING - 1 else i + 1, (u + 1) % RING)
                        n = u + 1 if first else 9
                        transpose_edges(*nxt, n)
                        edge_products(*nxt, n)
                    pe.wait_ge(s_msg, 2 * RING * i + 2 * u + 2)
                    sum_supertile(u)
            bodies(pe, message_body)

            def end_update(c, n, h, m):
                pe.wait_ge(s_d["z"], c + 1)
                if n >= 2:
                    pe.wait_ge(s_d["u"], c - 1)
                pe.matmul(banks[h][:, :], w_node[:, P:2 * P], cols(hT_all, c), start=True, stop=False)
                pe.matmul(banks[h][:, :], w_mean[:, :], z[:, h], start=False, stop=True).then_inc(s_d["mm"], 1)

            def end_tr(c, n, h, m):
                pe.wait_ge(s_d["u"], c + 1)
                if n >= 2:
                    pe.wait_ge(s_d["n"], c - 1)
                for k in range(CB):
                    last = pe.transpose(banks[2 + h][:, k * P:(k + 1) * P], hT[:, h, k * P:(k + 1) * P], ident[:, :])
                last.then_inc(s_d["tr"], 1)
            pe.wait_ge(s_msum, 2 * NS)
            pipeline(pe, (0, end_update), (2, end_tr))

        @block.vector
        def _(dve):
            next_norm = counter(dve, s_started_dve)
            dve.wait_ge(s_idx[0], 32)
            dve.tensor_copy(dst_f, dst_rows).then_inc(s_dve0, 1)
            dve.wait_ge(s_pool0, 7)
            dve.tensor_copy(iota_hist, bc_free(iota_i[:, :], HT))
            dve.tensor_copy(iota_w[:, :], iota_i[:, 0:W])
            dve.tensor_copy(window_off[:, :], window_i[:, :])
            dve.memset(count[:, :], 0.0).then_inc(s_iota, 1)

            dve.wait_ge(s_idxT, 1)
            for b, ps in enumerate(from_psum(0)):
                last = dve.tensor_copy(dst_col.rearrange("p (s j) -> p s j", j=TILES)[:, :, 4 * b:4 * b + 4], ps)
            last.then_inc(s_dstcol, 1)
            dve.wait_ge(s_dstcol, 1)
            dve.tensor_single_scalar(hi_i, dst_col, 7, ALU.arith_shift_right).then_inc(s_split, 1)
            dve.tensor_single_scalar(lo_i, dst_col, 127, ALU.bitwise_and).then_inc(s_split, 1)

            dve.wait_ge(s_iota, 1)
            dve.wait_ge(s_hilo, 2)

            def hist(g, h, wait):
                if wait:
                    dve.wait_ge(s_histmm, g - 1)
                dve.tensor_tensor(oh_lo[:, h], lo_col[:, bass.ds(g * HT, HT)].rearrange("p (o t) -> p o t", o=1).to_broadcast([P, P, HT]),
                                  iota_hist, ALU.is_equal)
                dve.tensor_tensor(oh_hi[:, h], hi_col[:, bass.ds(g * HT, HT)].rearrange("p (o t) -> p o t", o=1).to_broadcast([P, HI, HT]),
                                  iota_hist[:, 0:HI, :], ALU.is_equal).then_inc(s_hist, 1)
            hist(0, 0, False)
            hist(1, 1, False)
            with dve.Fori(1, LEAD) as i:
                hist(2 * i, 0, True)
                hist(2 * i + 1, 1, True)
            dve.wait_ge(s_std, 1)
            dve.reciprocal(rstd[:, :], rstd[:, :]).then_inc(s_rstd, 1)
            dve.wait_ge(s_rstd, 1)
            dve.tensor_tensor(nmr[:, :], neg_mean[:, :], rstd[:, :], ALU.mult).then_inc(s_rstd, 1)
            with dve.Fori(LEAD, GROUPS // 2) as i:
                hist(2 * i, 0, True)
                hist(2 * i + 1, 1, True)

            dve.wait_ge(s_histmm, GROUPS)
            dve.tensor_copy(count[:, 0:HI], banks[7][:, 0:HI]).then_inc(s_degree, 1)
            dve.wait_ge(s_degree, 1)
            dve.wait_ge(s_sdeg, 1)
            dve.reciprocal(dinv[:, :], dinv[:, :]).then_inc(s_small, 1)
            dve.wait_ge(s_small, 1)
            dve.wait_ge(s_u, NCH)

            def scale_rows(c, n, h, m):
                dve.tensor_tensor(blk(node_u, c), blk(node_u, c), bc_free(dinv[:, bass.ds(c * CB, CB)], P),
                                  ALU.mult).then_inc(s_t1, 1)
            chunks(dve, scale_rows)
            dve.tensor_single_scalar(rcount[:, :], count[:, :], 1.0, ALU.max).then_inc(s_small, 1)

            dve.tensor_reduce(base_span[:, 0:1], dst_f, AX.X, ALU.min).then_inc(s_red, 1)
            dve.wait_ge(s_srccol, 1)
            dve.scalar_tensor_tensor(src_f, dst_f, float(PAD_LIMIT), dst_f,
                                     ALU.is_lt, ALU.mult).then_inc(s_red, 1)
            dve.wait_ge(s_red, 2)
            dve.tensor_reduce(base_used[:, 0:1], src_f, AX.X, ALU.max).then_inc(s_red, 1)
            dve.wait_ge(s_red, 3)
            dve.tensor_tensor(base_span[:, 1:2], base_used[:, 0:1], base_span[:, 0:1], ALU.subtract).then_inc(s_span, 1)
            dve.wait_ge(s_small, 2)
            dve.reciprocal(rcount[:, :], rcount[:, :]).then_inc(s_small, 1)
            dve.wait_ge(s_base, 1)
            dve.tensor_reduce(span_max[:, :], banks[4][0:1, P:P + NS], AX.X, ALU.max).then_inc(s_small, 1)
            dve.wait_ge(s_small, 4)
            dve.tensor_single_scalar(is_banded[:, :], span_max[:, :], float(W) - 0.5, ALU.is_lt).then_inc(s_flag, 1)
            dve.wait_ge(s_flag, 1)
            dve.tensor_scalar(nwin_f[:, :], is_banded[:, :], float(1 - NW), float(NW), ALU.mult, ALU.add).then_inc(s_small, 1)
            dve.tensor_scalar(base_row_f[:, :], banks[4][0:1, 0:NS], is_banded[0:1, 0:1], None, ALU.mult).then_inc(s_small, 1)
            dve.wait_ge(s_small, 6)
            dve.tensor_copy(nwin_i[:, :], nwin_f[:, :]).then_inc(s_small, 1)
            dve.tensor_copy(base_row[:, :], base_row_f[:, :]).then_inc(s_small, 1)
            dve.wait_ge(s_band, 1)
            dve.tensor_tensor(base_used[:, :], banks[5][0:NS, 0:1], base_span[:, 0:1], ALU.mult).then_inc(s_red, 1)
            dve.wait_ge(s_red, 4)
            dve.tensor_scalar(dst_f, dst_f, base_used[:, 0:1], None, ALU.subtract).then_inc(s_rel, 1)
            dve.wait_ge(s_relT, 1)
            for b, ps in enumerate(from_psum(4)):
                last = dve.tensor_copy(rel_col[:, :, 4 * b:4 * b + 4], ps)
            last.then_inc(s_relcol, 1)

            def diagonals(ph, value):
                def diagonal(c, n, h, m):
                    if ph or n >= 2:
                        dve.wait_ge(s_dbc, ph * NCH + (c - 1 if n >= 2 else 0))
                    dve.tensor_tensor(q3(z[:, h]), bc_mid(ident[:, :], CB), bc_free(value[:, bass.ds(c * CB, CB)], P),
                                      ALU.mult).then_inc(s_diag, 1)
                chunks(dve, diagonal)

            def add_b2(c, n, h, m):
                dve.tensor_tensor(blk(x_sb, c), blk(x_sb, c), bc_mid(b2_bc[:, :], CB), ALU.add).then_inc(s_xb, 1)
            diagonals(0, dinv)

            dve.wait_ge(s_small, 8)
            dve.wait_ge(s_relcol, 1)
            nwin = dve.value_load(nwin_i[0:1, 0:1], min_val=1, max_val=NW)
            done = dve.alloc_register("windows_dve")
            dve.reg_mov(done, 0)

            def sum_supertile(s):
                base = dve.value_load(base_row[0:1, bass.ds(s, 1)], min_val=0, max_val=N - 1)
                with dve.Fori(0, nwin) as k:
                    dve.reg_add(done, done, 1)
                    d = dve.snap(done)
                    dve.scalar_tensor_tensor(oh[:, :, :], rel_col[:, bass.ds(s, 1), :].rearrange("p s (j o) -> p (s j) o", o=1).to_broadcast([P, TILES, W]),
                                             window_off[:, bass.ds(k, 1)], bc_mid(iota_w[:, :], TILES),
                                             ALU.subtract, ALU.is_equal).then_inc(s_oh, 1)
                    start = nc.s_assert_within(base + k * W, 0, NP - W, skip_runtime_bounds_check_because="base is 0 where k is above 0")
                    dve.wait_ge(s_agg, d)
                    dve.tensor_tensor(acc[:, bass.ds(start, W)], acc[:, bass.ds(start, W)], banks[6][:, 0:W],
                                      ALU.add).then_inc(s_added, 1)
                    dve.wait_ge(s_added, d)
                dve.sem_inc(s_free, 1)

            def gcn_phase(ph):
                dve.wait_ge(s_acc0, NCH * (ph + 1))
                with dve.Fori(0, BODIES) as i:
                    for u in range(RING):
                        sum_supertile(RING * i + u)
            gcn_phase(0)

            dve.wait_ge(s_dbcc, NCH)

            def second_z(c, n, h, m):
                if n >= 2:
                    dve.wait_ge(s_zw, c - 1)
                dve.tensor_tensor(z[:, h], cols(acc, c), cols(dinv_bc, c), ALU.mult).then_inc(s_z, 1)

            def second_table(c, n, h, m):
                dve.wait_ge(s_zw, c + 1)
                if n >= 2:
                    dve.wait_ge(s_tab[h], 16 * m + STORES[h])
                    dve.wait_ge(s_selfT, NCH + c - 1)
                dve.tensor_tensor(q3(st[:, h]), q3(banks[h][:, :]), bc_free(dinv[:, bass.ds(c * CB, CB)], P),
                                  ALU.mult).then_inc(s_t, 1)
            pipeline(dve, (0, second_z), (2, second_table))
            diagonals(1, rcount)
            chunks(dve, add_b2)
            gcn_phase(1)

            def norms(c, sems, rows, h):
                next_norm()
                for k in range(CB):
                    dve.bn_stats(stats[:, h, k, :], rows(k)).then_inc(sems["bn"], 1)
                dve.wait_ge(sems["bn"], 2 * CB * c + CB)
                next_norm()
                for k in range(CB):
                    dve.bn_aggr(cmv[:, h, k, :], stats[:, h, k, :]).then_inc(sems["bn"], 1)

            def scales(c, n, sems, used, h):
                if n >= 2:
                    dve.wait_ge(sems[used], c - 1)
                dve.wait_ge(sems["std"], c + 1)
                dve.reciprocal(crstd[:, h], cstd[:, h]).then_inc(sems["rstd"], 1)
                dve.wait_ge(sems["rstd"], 2 * c + 1)
                dve.scalar_tensor_tensor(cnmr[:, h], cmv[:, h, :, 0], -1.0, crstd[:, h],
                                         ALU.mult, ALU.mult).then_inc(sems["rstd"], 1)

            def third_x2(c, n, h, m):
                dve.wait_ge(s_c["tr"], c + 1)
                dve.tensor_tensor(blk(x_sb, c), q3(banks[h][:, :]), blk(x_sb, c), ALU.add).then_inc(s_c["x2"], 1)
                dve.wait_ge(s_c["x2"], c + 1)
                norms(c, s_c, lambda k: x_sb[:, c * CB + k, :], h)

            def third_scales(c, n, h, m):
                scales(c, n, s_c, "h", h)

            def third_table(c, n, h, m):
                dve.wait_ge(s_c["hw"], c + 1)
                if n >= 2:
                    dve.wait_ge(s_tab[h], 16 * m + 2 * STORES[h])
                dve.tensor_tensor(q3(st[:, h]), q3(banks[4 + h][:, :]), bc_mid(bmsg_bc[:, :], CB),
                                  ALU.add).then_inc(s_c["t3"], 1)
            pipeline(dve, (0, third_x2), (5, third_table), (1, third_scales))

            dve.wait_ge(s_c["z"], NCH)
            dve.memset(acc[:, :], 0.0).then_inc(s_zero, 1)
            dve.wait_ge(s_zero, 1)

            def message_body(i, first, last):
                for u in range(RING):
                    dve.wait_ge(s_g[u], 16 * TILES * i + 16 * TILES * (2 * BODIES + 1))
                    for half in range(2):
                        dve.wait_ge(s_m, 2 * RING * i + 2 * u + half + 1)
                        rows = G[:, u, 4 * half:4 * half + 4, :]
                        dve.tensor_tensor(rows, q3(banks[2 + 2 * (u % 2) + half][:, :]), rows, ALU.add).then_inc(s_msum, 1)
                    sum_supertile(RING * i + u)
            bodies(dve, message_body)

            def end_norms(c, n, h, m):
                dve.wait_ge(s_d["tr"], c + 1)
                norms(c, s_d, lambda k: banks[2 + h][:, k * P:(k + 1) * P], h)

            def end_scales(c, n, h, m):
                scales(c, n, s_d, "n", h)

            def end_rows(c, n, h, m):
                dve.wait_ge(s_d["g"], c + 1)
                if n >= 2:
                    dve.wait_ge(s_out[h], 16 * m)
                dve.tensor_tensor(q3(y[:, h]), q3(st[:, h]), blk(hb_all, c), ALU.add).then_inc(s_d["b"], 1)
                dve.wait_ge(s_d["b"], c + 1)
                dve.scalar_tensor_tensor(y[:, h], y[:, h], 0.0, blk(x_sb, c).rearrange("p k f -> p (k f)"),
                                         ALU.max, ALU.add).then_inc(s_d["fin"], 1)
            dve.wait_ge(s_c["hb"], NCH)
            pipeline(dve, (6, end_rows), (4, end_scales), (3, end_norms))


_INS = ["x", "src", "dst", "edge_attr_128", "L0_gnn_W1", "L0_gnn_b1", "L0_gnn_W2", "L0_gnn_b2",
        "L1_gnn_W_msg", "L1_gnn_b_msg", "L1_gnn_W_upd", "L1_gnn_b_upd", "L1_gnn_gamma", "L1_gnn_beta"]


def kernel(**inputs):
    import numpy as _np
    import concourse.bacc as _bacc
    from concourse import mybir as _mybir
    from concourse.bass_utils import run_bass_kernel_spmd as _run

    nc = _bacc.Bacc("TRN2", target_bir_lowering=False, num_devices=1)
    arrays, args = {}, []
    for name in _INS:
        a = _np.ascontiguousarray(inputs[name])
        arrays[f"in_{name}"] = a
        args.append(nc.dram_tensor(f"in_{name}", a.shape, _mybir.dt.from_np(a.dtype), kind="ExternalInput").ap())
    shape = inputs["x"].shape
    args.append(nc.dram_tensor("out_x", tuple(shape), _mybir.dt.float32, kind="ExternalOutput").ap())
    gnn_program(nc, *args)
    r = _run(nc, [arrays], core_ids=[0])
    return r.results[0]["out_x"]
```

```python
import concourse.bass as bass
from concourse import mybir
from contextlib import ExitStack

P = 128
TILES = 8
W = 96
RING = 4
CB = 4
CH = CB * P
HT = 16
LO = 64
PAD_DST = 16384
PAD_LIMIT = 8192
EPS = 1e-5


def gnn_program(nc, x, src, dst, edge, W1, b1, W2, b2, W_msg, b_msg, W_upd, b_upd, gamma, beta, out):
    f32, i32, bf16 = mybir.dt.float32, mybir.dt.int32, mybir.dt.bfloat16
    ALU, ACT, AX = mybir.AluOpType, mybir.ActivationFunctionType, mybir.AxisListType

    N = x.shape[0]
    E = src.shape[0]
    SE = P * TILES
    NS = -(-E // (SE * RING)) * RING
    FULL = E // SE
    LAST = E - FULL * SE
    assert NS == FULL + 1 and LAST > 0 and NS <= P
    BODIES = NS // RING
    NCH = -(-N // CH)
    NB = NCH * CB
    NP = NB * P
    assert NCH >= 5 and NS == 2 * RING * NCH
    XB = N // P
    XR = N - XB * P
    HALF_TILES = TILES // 2
    HI = -(-N // P)
    HALF = (NCH - 2) * CB
    TAIL = HI - (NCH - 1) * CB
    UNITS = NCH + 1
    NW = -(-N // W)
    assert NW * W <= NP and N - 1 + W <= NP and N < PAD_LIMIT
    HV = 2 * HI
    assert P == 2 * LO and HV <= P
    GROUPS = NS * TILES // HT
    assert GROUPS % 2 == 0 and GROUPS >= 6

    tables = [nc.dram_tensor(f"table{n}", (HI * P, P), f32, kind="Internal").ap() for n in range(2)]

    ctx = ExitStack()
    with ctx:
        def sb(name, shape, dt=f32):
            return ctx.enter_context(nc.sbuf_tensor(name, shape, dt))

        def sem(name):
            return ctx.enter_context(nc.semaphore(name))

        w1 = sb("w1", [P, P])
        w2 = sb("w2", [P, P])
        w_node = sb("w_node", [P, 2 * P])
        w_edge = sb("w_edge", [P, P])
        w_mean = sb("w_mean", [P, P])
        b1_col = sb("b1_col", [P, 1])
        b2_bc = sb("b2_bc", [P, P])
        bmsg_bc = sb("bmsg_bc", [P, P])
        bupd_col = sb("bupd_col", [P, 1])
        gamma_bc = sb("gamma_bc", [P, P])
        beta_bc = sb("beta_bc", [P, P])
        ident = sb("ident", [P, P])
        ones = sb("ones", [P, P])
        zeros = sb("zeros", [P, CH])
        iota_i = sb("iota_i", [P, P], i32)
        iota_w = sb("iota_w", [P, W])
        window_i = sb("window_i", [P, NW], i32)
        window_off = sb("window_off", [P, NW])
        least_i = sb("least_i", [NS, 1], i32)
        least_f = sb("least_f", [NS, 1])
        early = sb("early", [NS, 1])
        eps_col = sb("eps_col", [P, 1])

        src_col = sb("src_col", [P, NS, TILES], i32)
        rel_col = sb("rel_col", [P, NS, TILES])
        base_span = sb("base_span", [NS, 2])
        base_row_f = sb("base_row_f", [1, NS])
        base_row = sb("base_row", [1, NS], i32)
        span_max = sb("span_max", [1, 1])
        is_banded = sb("is_banded", [1, 1])
        nwin_f = sb("nwin_f", [1, 1])
        nwin_i = sb("nwin_i", [1, 1], i32)
        base_used = sb("base_used", [NS, 1])

        x_sb = sb("x_sb", [P, NB, P])
        acc = sb("acc", [P, NP])
        dinv_bc = sb("dinv_bc", [P, NP])
        rc_bc = sb("rc_bc", [P, NP])
        node_u = sb("node_u", [P, NB, P])
        hT_all = node_u[:, :, :].rearrange("p b f -> p (b f)")
        hb_all = dinv_bc[:, :].rearrange("p (b f) -> p b f", f=P)
        count = sb("count", [P, NB])
        dinv = sb("dinv", [P, NB])
        rcount = sb("rcount", [P, NB])
        neg_mean = sb("neg_mean", [P, NB])
        sq_sum = sb("sq_sum", [P, NB])
        rstd = sb("rstd", [P, NB])
        nmr = sb("nmr", [P, NB])

        acc_bf = acc[:, :].bitcast(bf16)
        VALUES = max(LO, HV)
        assert (VALUES + 2 * LO + 2 * P) * HT <= 2 * NP
        iota_hist = acc_bf[:, 0:VALUES * HT].rearrange("p (v t) -> p v t", t=HT)
        one_hots = acc_bf[:, VALUES * HT:(VALUES + 2 * LO + 2 * P) * HT]
        oh_lo = one_hots[:, 0:2 * LO * HT].rearrange("p (h v t) -> p h v t", h=2, t=HT)
        oh_hi = one_hots[:, 2 * LO * HT:].rearrange("p (h v t) -> p h v t", h=2, t=HT)
        C = NS * TILES
        assert 4 * C <= NP
        dst_col, hi_i, lo_i = [dinv_bc[:, n * C:(n + 1) * C].bitcast(i32) for n in range(3)]
        hilo = dinv_bc[:, 3 * C:4 * C].bitcast(bf16)
        hi_col, lo_col = hilo[:, 0:C], hilo[:, C:2 * C]

        G = sb("G", [P, RING, TILES, P])
        edges = sb("edges", [P, RING, TILES, P])
        dst_rows, src_rows, dst_f, src_f = [edges[0:NS, u].rearrange("s j f -> s (j f)") for u in range(4)]
        dst_rows, src_rows = dst_rows.bitcast(i32), src_rows.bitcast(i32)
        idx_ring = sb("idx_ring", [P, RING, TILES], i32)
        edgeT = sb("edgeT", [P, 2, CH])
        oh = sb("oh", [P, 2, TILES, W])
        z = sb("z", [P, 2, CH])
        st = sb("st", [P, 2, CH])
        hT = sb("hT", [P, 2, CH])
        y = sb("y", [P, 2, CH])
        halves = y[0:HV, 0, 0:2 * P].rearrange("p (q f) -> p q f", q=2)
        stats = sb("stats", [P, 2, CB, 6])
        cmv = sb("cmv", [P, 2, CB, 2])
        cstd = sb("cstd", [P, 2, CB])
        crstd = sb("crstd", [P, 2, CB])
        cnmr = sb("cnmr", [P, 2, CB])

        banks = [ctx.enter_context(nc.psum_tensor(f"bank{i}", [P, 512], f32)) for i in range(8)]

        s_loads = sem("s_loads")
        s_x = sem("s_x")
        s_idx = [sem("s_idx_dst"), sem("s_idx_src")]
        s_pool0 = sem("s_pool0")
        s_dve0 = sem("s_dve0")
        s_pad = sem("s_pad")
        s_idxT = sem("s_idxT")
        s_base = sem("s_base")
        s_band = sem("s_band")
        s_relT = sem("s_relT")
        s_hist = sem("s_hist")
        s_histmm = sem("s_histmm")
        s_halves = sem("s_halves")
        s_count = sem("s_count")
        s_std = sem("s_std")
        s_rstd = sem("s_rstd")
        s_sdeg = sem("s_sdeg")
        s_h = sem("s_h")
        s_hTp = sem("s_hTp")
        s_hTc = sem("s_hTc")
        s_hw = sem("s_hw")
        s_u = sem("s_u")
        s_t1 = sem("s_t1")
        s_stored = sem("s_stored")
        s_selfT = sem("s_selfT")
        s_acc0 = sem("s_acc0")
        s_diag = sem("s_diag")
        s_dbc = sem("s_dbc")
        s_dbcc = sem("s_dbcc")
        s_xb = sem("s_xb")
        s_idxr = sem("s_idxr")
        s_g = [[sem(f"s_g{u}_{q}") for q in range(2)] for u in range(RING)]
        s_free = sem("s_free")
        s_oh = sem("s_oh")
        s_agg = sem("s_agg")
        s_added = sem("s_added")
        s_z = sem("s_z")
        s_zr = sem("s_zr")
        s_zw = sem("s_zw")
        s_t = sem("s_t")
        s_c = {n: sem("s_c_" + n) for n in
               ("z", "tr", "zero", "x2", "bn", "std", "rstd", "h", "hT", "hTc", "hTa", "hw", "t3", "hb")}
        s_started_pool = sem("s_started_pool")
        s_started_pe = sem("s_started_pe")
        s_started_dve = sem("s_started_dve")
        s_mean = sem("s_mean")
        s_sq = sem("s_sq")
        s_srcf = sem("s_srcf")
        s_hilo = sem("s_hilo")
        s_degree = sem("s_degree")
        s_srccol = sem("s_srccol")
        s_dstcol = sem("s_dstcol")
        s_split = sem("s_split")
        s_iota = sem("s_iota")
        s_red = sem("s_red")
        s_span = sem("s_span")
        s_small = sem("s_small")
        s_flag = sem("s_flag")
        s_rel = sem("s_rel")
        s_relcol = sem("s_relcol")
        s_own = sem("s_own")
        s_e = [sem(f"s_e{u}") for u in range(RING)]
        s_eT = sem("s_eT")
        s_eTc = sem("s_eTc")
        s_m = sem("s_m")
        s_msum = sem("s_msum")
        s_msg = sem("s_msg")
        s_d = {n: sem("s_d_" + n) for n in
               ("z", "mm", "u", "tr", "bn", "std", "rstd", "n", "g", "b", "fin")}
        s_started_act = sem("s_started_act")

        end_banks = [banks[7], banks[0]]

        block = ctx.enter_context(nc.Block())

        def bc_free(ap, n):
            return ap.rearrange("p (k o) -> p k o", o=1).to_broadcast([ap.shape[0], ap.shape[1], n])

        def bc_mid(ap, k):
            return ap.rearrange("p (o n) -> p o n", o=1).to_broadcast([ap.shape[0], k, ap.shape[1]])

        def node_cols(ap, b, blocks):
            return ap[:, bass.ds(b * P, blocks * P)]

        def node_blocks(ap, b, blocks):
            return ap[:, bass.ds(b, blocks)]

        def chunk_cols(ap, c):
            return node_cols(ap, c * CB, CB)

        def chunk_blocks(ap, c):
            return node_blocks(ap, c * CB, CB)

        def q3(ap):
            return ap.rearrange("p (k f) -> p k f", f=P)

        def pipeline(eng, *steps, peel=0):
            lags = [lag for lag, _ in steps]

            def turn(t):
                for lag, step in steps:
                    c = t - lag
                    if 0 <= c < NCH:
                        step(c, c, c % 2, c // 2)
            first = max(lags) + 2
            pairs = max(0, (NCH - first - peel) // 2)
            if pairs < 2:
                pairs = 0
            for t in range(first if pairs else NCH + max(lags)):
                turn(t)
            if pairs:
                with eng.Fori(1, pairs + 1) as i:
                    for b in range(2):
                        for lag, step in steps:
                            at = first - 2 + b - lag
                            step(2 * i + at, 2, at % 2, i + at // 2)
                for t in range(first + 2 * pairs, NCH + max(lags)):
                    turn(t)

        def chunks(eng, step):
            pipeline(eng, (0, step))

        def gather_loop(eng, body, fast=None, steps=()):
            def unit(n, b, blocks):
                for step in steps:
                    step(n, b, 0, blocks)

            body(0, True, False)
            body(1, False, False)
            if steps:
                with eng.If(fast == 1):
                    with eng.Fori(1, NCH - 1) as j:
                        body(2 * j, False, False)
                        body(2 * j + 1, False, False)
                        unit(j - 1, CB * j - CB, CB)
                    body(BODIES - 2, False, False)
                    unit(NCH - 2, HALF, CB // 2)
                with eng.Else():
                    with eng.Fori(2, BODIES - 1) as i:
                        body(i, False, False)
            else:
                with eng.Fori(2, BODIES - 1) as i:
                    body(i, False, False)
            body(BODIES - 1, False, True)
            if steps:
                with eng.If(fast != 1):
                    with eng.Fori(0, NCH - 2) as n:
                        unit(n, CB * n, CB)
                    unit(NCH - 2, HALF, CB // 2)
                for step in steps:
                    step(NCH - 1, HALF + CB // 2, 0, CB // 2)
                    step(NCH, (NCH - 1) * CB, 1, TAIL)

        def counter(eng, started):
            return lambda: eng.sem_inc(started, 1)

        def table_rows(ph, b, blocks):
            return tables[ph % 2][bass.ds(b * P, blocks * P), :].rearrange("(k p) f -> p k f", p=P)

        LEAD = GROUPS // 2 - NCH + 1
        assert LEAD >= 2
        N_WEIGHTS = 6
        N_BIASES = 6

        def from_psum(b):
            return [banks[b + h][:, :].rearrange("p (j s) -> p s j", s=P)[:, 0:NS, :] for h in range(2)]

        @block.sync
        def _(sp):
            sp.wait_ge(s_pad, 1)
            rows = FULL * SE
            sp.dma_start(dst_rows[0:FULL, :], dst[0:rows].rearrange("(s e) -> s e", e=SE)).then_inc(s_idx[0], 16)
            sp.dma_start(dst_rows[FULL:NS, SE - LAST:SE], dst[rows:E].rearrange("(s e) -> s e", s=1)).then_inc(s_idx[0], 16)
            sp.dma_start(src_rows[0:FULL, :], src[0:rows].rearrange("(s e) -> s e", e=SE)).then_inc(s_idx[1], 16)
            sp.dma_start(src_rows[FULL:NS, :], src[E - SE:E].rearrange("(s e) -> s e", s=1)).then_inc(s_idx[1], 16)
            sp.wait_ge(s_pad, 2)
            sp.dma_start(x_sb[:, 0:XB, :], x[0:XB * P, :].rearrange("(b p) f -> p b f", p=P)).then_inc(s_x, 16)
            sp.dma_start(x_sb[0:XR, XB, :], x[XB * P:N, :]).then_inc(s_x, 16)

            def load_edges(i, u, row, wait):
                if wait:
                    sp.wait_ge(s_eT, 2 * RING * i - 2 * RING + 2 * u + 2)
                sp.dma_start(edges[:, u, :, :].rearrange("p j f -> p (j f)"),
                             edge[row, :].rearrange("(p j) f -> p (j f)", p=P)).then_inc(s_e[u], 16)

            def store_scaled(c, n, h, m):
                sp.wait_ge(s_t1, c + 1)
                blocks = TAIL if n == NCH - 1 else CB
                sp.dma_start(table_rows(0, c * CB, blocks), node_blocks(node_u, c * CB, blocks)).then_inc(s_stored, 16)
            pipeline(sp, (0, store_scaled), peel=1)

            sp.wait_ge(s_relT, 1)
            sp.wait_ge(s_red, 6)
            for u in range(RING):
                load_edges(0, u, slice(u * SE, (u + 1) * SE), False)

            with sp.Fori(1, BODIES - 1) as i:
                for u in range(RING):
                    load_edges(i, u, bass.ds(i * (RING * SE) + u * SE, SE), True)
            i = BODIES - 1
            for u in range(RING):
                s = i * RING + u
                row = min(s * SE, E - SE)
                load_edges(i, u, slice(row, row + SE), True)
            sp.wait_ge(s_stored, 16 * (NCH + 2 * UNITS + NCH + TAIL))

        @block.gpsimd
        def _(pool):
            pool.memset(dst_rows[:, :], PAD_DST).then_inc(s_pad, 1)
            pool.memset(x_sb[:, XB:NB, :], 0.0).then_inc(s_pad, 1)
            pool.iota(iota_i[:, :], pattern=[[1, P]], base=0, channel_multiplier=0).then_inc(s_pool0, 1)
            pool.iota(window_i[:, :], pattern=[[W, NW]], base=0, channel_multiplier=0).then_inc(s_pool0, 1)
            pool.iota(least_i[:, :], pattern=[[0, 1]], base=-CH, channel_multiplier=CH // (2 * RING)).then_inc(s_pool0, 1)
            pool.memset(ident[:, :], 0.0).then_inc(s_pool0, 1)
            pool.wait_ge(s_pool0, 4)
            pool.affine_select(out=ident[:, :], in_=ident[:, :], compare_op=ALU.not_equal, fill=1.0,
                               base=0, pattern=[[-1, P]], channel_multiplier=1).then_inc(s_pool0, 1)
            pool.memset(ones[:, :], 1.0).then_inc(s_pool0, 1)
            pool.memset(zeros[:, :], 0.0).then_inc(s_pool0, 1)
            pool.memset(halves, 0.0).then_inc(s_pool0, 1)
            pool.memset(oh_hi[:, :, HV:P, :], 0.0).then_inc(s_pool0, 1)
            pool.memset(eps_col[:, :], EPS).then_inc(s_pool0, 1)

            next_supertile = counter(pool, s_started_pool)

            def gather_phase(ph):
                def body(i, first, last):
                    for u in range(RING):
                        if not (ph == 0 and first):
                            pool.wait_ge(s_free, RING * i + (ph * NS + u - RING + 1))
                        pool.wait_ge(s_idxr, RING * i + (ph * NS + u + 1))
                        pool.wait_ge(s_stored, 16 * (NCH + UNITS * ph))
                        next_supertile()
                        for j in range(TILES):
                            pool.indirect_dma_start(
                                out=G[:, u, j, :], out_offset=None, in_=tables[ph % 2],
                                in_offset=bass.IndirectOffsetOnAxis(ap=idx_ring[:, u, j:j + 1], axis=0),
                            ).then_inc(s_g[u][j // HALF_TILES], 16)
                gather_loop(pool, body)
            for ph in range(3):
                gather_phase(ph)

        @block.scalar
        def _(act):
            for dram, tile in ((W1, w1[:, :]), (W2, w2[:, :]),
                               (W_msg[0:P, :], w_node[:, 0:P]), (W_upd[0:P, :], w_node[:, P:2 * P]),
                               (W_msg[P:2 * P, :], w_edge[:, :]), (W_upd[P:2 * P, :], w_mean[:, :])):
                act.dma_start(tile, dram).then_inc(s_loads, 16)
            for dram, tile in ((b1, b1_col), (b_upd, bupd_col)):
                act.dma_start(tile[:, :], dram.rearrange("(p o) -> p o", o=1)).then_inc(s_loads, 16)
            for dram, tile in ((b2, b2_bc), (b_msg, bmsg_bc), (gamma, gamma_bc), (beta, beta_bc)):
                act.dma_start(tile[:, :], dram.rearrange("(o f) -> o f", o=1).to_broadcast([P, P])).then_inc(s_loads, 16)

            act.wait_ge(s_idx[1], 32)
            act.activation(src_f, src_rows, ACT.Copy).then_inc(s_srcf, 1)
            act.wait_ge(s_idxT, 2)
            for b, ps in enumerate(from_psum(2)):
                last = act.activation(src_col[:, :, 4 * b:4 * b + 4], ps, ACT.Copy)
            last.then_inc(s_srccol, 1)

            act.wait_ge(s_pool0, 10)
            act.wait_ge(s_x, 32)

            def first_mean(c, n, h, m):
                for k in range(CB):
                    last = act.activation(node_u[:, bass.ds(c * CB + k, 1), :], x_sb[:, bass.ds(c * CB + k, 1), :],
                                          ACT.Copy, scale=-1.0 / P,
                                          accum_out=neg_mean[:, bass.ds(c * CB + k, 1)])
                last.then_inc(s_mean, 1)

            def first_squares(c, n, h, m):
                act.wait_ge(s_mean, c + 1)
                for k in range(CB):
                    last = act.activation(rc_bc[:, bass.ds((c * CB + k) * P, P)], x_sb[:, c * CB + k, :], ACT.Square,
                                          bias=neg_mean[:, bass.ds(c * CB + k, 1)],
                                          accum_out=sq_sum[:, bass.ds(c * CB + k, 1)])
                last.then_inc(s_sq, 1)
            pipeline(act, (0, first_mean), (1, first_squares))
            act.wait_ge(s_sq, NCH)
            act.activation(rstd[:, :], sq_sum[:, :], ACT.Sqrt, scale=1.0 / P, bias=eps_col[:, 0:1]).then_inc(s_std, 1)
            act.wait_ge(s_rstd, 2)

            def first_h(c, n, h, m):
                if n >= 2:
                    act.wait_ge(s_hTp, c - 1)
                for k in range(CB):
                    last = act.activation(z[:, h, k * P:(k + 1) * P], x_sb[:, c * CB + k, :], ACT.Relu,
                                          scale=rstd[:, bass.ds(c * CB + k, 1)], bias=nmr[:, bass.ds(c * CB + k, 1)])
                last.then_inc(s_h, 1)

            def first_hT(c, n, h, m):
                act.wait_ge(s_hTp, c + 1)
                if n >= 2:
                    act.wait_ge(s_hw, c - 1)
                act.activation(hT[:, h], banks[h][:, :], ACT.Copy).then_inc(s_hTc, 1)

            def first_hw(c, n, h, m):
                act.wait_ge(s_hw, c + 1)
                act.activation(chunk_blocks(node_u, c), q3(banks[2 + h][:, :]), ACT.Copy).then_inc(s_u, 1)

            def degree_root(c, n, h, m):
                if n == NCH - 2:
                    act.wait_ge(s_degree, 1)
                    act.activation(dinv[:, :], count[:, :], ACT.Sqrt, bias=ones[:, 0:1]).then_inc(s_sdeg, 1)
            pipeline(act, (0, first_h), (1, degree_root), (1, first_hT), (2, first_hw), peel=2)

            def fill_indices(ph, i, u, first):
                if not (ph == 0 and first):
                    for half in range(2):
                        act.wait_ge(s_g[u][half], 16 * HALF_TILES * i + 16 * HALF_TILES * BODIES * ph)
                act.activation(idx_ring[:, u, :], src_col[:, RING * i + u, :], ACT.Copy).then_inc(s_idxr, 1)

            act.wait_ge(s_srccol, 1)
            for u in range(RING):
                fill_indices(0, 0, u, True)

            def copy_own(c, n, h, m):
                act.wait_ge(s_t1, c + 1)
                if n >= 2:
                    act.wait_ge(s_selfT, c - 1)
                act.activation(q3(st[:, h]), chunk_blocks(node_u, c), ACT.Copy).then_inc(s_own, 1)

            def own_rows(c, n, h, m):
                act.wait_ge(s_selfT, c + 1)
                act.activation(chunk_cols(acc, c), banks[h][:, :], ACT.Copy).then_inc(s_acc0, 1)
            pipeline(act, (0, copy_own), (2, own_rows))

            def broadcasts(ph, rows):
                def broadcast_rows(c, n, h, m):
                    act.wait_ge(s_dbc, ph * NCH + c + 1)
                    act.activation(chunk_cols(rows, c), banks[2 + h][:, :], ACT.Copy).then_inc(s_dbcc, 1)
                chunks(act, broadcast_rows)
            broadcasts(0, dinv_bc)

            def next_indices(ph, i, u, last):
                if not last:
                    fill_indices(ph, i + 1, u, False)
                elif ph < 2:
                    fill_indices(ph + 1, 0, u, True)

            def gcn_phase(ph, *steps):
                def body(i, first, last):
                    for u in range(RING):
                        next_indices(ph, i, u, last)
                gather_loop(act, body, nwin, steps)

            def store_table(ph, ready):
                def store(n, b, h, blocks):
                    act.wait_ge(ready, n + 1)
                    next_store()
                    act.dma_start(table_rows(ph, b, blocks), q3(st[:, h, 0:blocks * P])).then_inc(s_stored, 16)
                return store
            act.wait_ge(s_small, 8)
            nwin = act.value_load(nwin_i[0:1, 0:1], min_val=1, max_val=NW)
            next_store = counter(act, s_started_act)

            def second_z(n, b, h, blocks):
                act.wait_ge(s_z, n + 1)
                act.activation(z[:, h, 0:blocks * P], z[:, h, 0:blocks * P], ACT.Relu, bias=b1_col[:, 0:1]).then_inc(s_zr, 1)

            def second_own(n, b, h, blocks):
                act.wait_ge(s_selfT, NCH + n + 1)
                act.activation(node_cols(acc, b, blocks), banks[2 + h][:, 0:blocks * P], ACT.Copy).then_inc(s_acc0, 1)
            gcn_phase(0, second_z, store_table(1, s_t), second_own)
            broadcasts(1, rc_bc)

            def third_std(n, b, h, blocks):
                act.wait_ge(s_c["bn"], 2 * b + 2 * blocks)
                act.activation(cstd[:, h, 0:blocks], cmv[:, h, 0:blocks, 1], ACT.Sqrt, bias=eps_col[:, 0:1]).then_inc(s_c["std"], 1)

            def third_h(n, b, h, blocks):
                act.wait_ge(s_c["rstd"], 2 * n + 2)
                for k in range(blocks):
                    last = act.activation(y[:, h, k * P:(k + 1) * P], x_sb[:, b + k, :], ACT.Relu,
                                          scale=crstd[:, h, k:k + 1], bias=cnmr[:, h, k:k + 1])
                last.then_inc(s_c["h"], 1)

            def third_hT(n, b, h, blocks):
                act.wait_ge(s_c["hT"], n + 1)
                act.activation(hT[:, h, 0:blocks * P], banks[2 + h][:, 0:blocks * P], ACT.Copy).then_inc(s_c["hTc"], 1)

            def third_keep(n, b, h, blocks):
                act.activation(node_cols(hT_all, b, blocks), banks[2 + h][:, 0:blocks * P], ACT.Copy).then_inc(s_c["hTa"], 1)
            gcn_phase(1, third_std, third_h, third_hT, third_keep, store_table(2, s_c["t3"]))

            def copy_edges(i, u, first):
                for half in range(2):
                    n = 2 * RING * i + 2 * u + half
                    act.wait_ge(s_eT, n + 1)
                    if not first:
                        act.wait_ge(s_m, n - 1)
                    act.activation(edgeT[:, half], banks[half][:, :], ACT.Copy).then_inc(s_eTc, 1)

            copy_edges(0, 0, True)

            def message_body(i, first, last):
                for u in range(RING):
                    if not (last and u == RING - 1):
                        copy_edges(i if u < RING - 1 else i + 1, (u + 1) % RING, False)
                    for half in range(2):
                        act.wait_ge(s_msum, 2 * RING * i + 2 * u + half + 1)
                        act.activation(G[:, u, 4 * half:4 * half + 4, :], G[:, u, 4 * half:4 * half + 4, :],
                                       ACT.Relu).then_inc(s_msg, 1)
                    next_indices(2, i, u, last)

            def end_update(n, b, h, blocks):
                act.wait_ge(s_d["mm"], n + 1)
                act.activation(hT[:, h, 0:blocks * P], end_banks[h][:, 0:blocks * P], ACT.Identity, bias=bupd_col[:, 0:1]).then_inc(s_d["u"], 1)

            def end_std(n, b, h, blocks):
                act.wait_ge(s_d["bn"], 2 * b + 2 * blocks)
                act.activation(cstd[:, h, 0:blocks], cmv[:, h, 0:blocks, 1], ACT.Sqrt, bias=eps_col[:, 0:1]).then_inc(s_d["std"], 1)

            def end_norm(n, b, h, blocks):
                act.wait_ge(s_d["rstd"], 2 * n + 2)
                for k in range(blocks):
                    last = act.activation(st[:, h, k * P:(k + 1) * P], end_banks[h][:, k * P:(k + 1) * P], ACT.Identity,
                                          scale=crstd[:, h, k:k + 1], bias=cnmr[:, h, k:k + 1])
                last.then_inc(s_d["n"], 1)

            def store_out(n, b, h, blocks):
                act.wait_ge(s_d["fin"], n + 1)
                next_store()
                if h == 0:
                    act.dma_start(out[bass.ds(b * P, blocks * P), :].rearrange("(k p) f -> p k f", p=P),
                                  q3(y[:, h, 0:blocks * P])).then_inc(s_stored, 16)
                else:
                    for k in range(blocks):
                        row = (b + k) * P
                        n = min(P, N - row)
                        act.dma_start(out[row:row + n, :], y[0:n, h, k * P:(k + 1) * P]).then_inc(s_stored, 16)
            gather_loop(act, message_body, nwin, (end_update, end_std, end_norm, store_out))

        @block.tensor
        def _(pe):
            pe.wait_ge(s_pool0, 10)
            pe.wait_ge(s_dve0, 1)
            for j in range(TILES):
                last = pe.transpose(banks[j // 4][:, (j % 4) * P:(j % 4) * P + NS],
                                    dst_f[:, :].rearrange("s (p j) -> s p j", j=TILES)[:, :, j],
                                    ident[0:NS, 0:NS])
            last.then_inc(s_idxT, 1)
            pe.wait_ge(s_srcf, 1)
            for j in range(TILES):
                last = pe.transpose(banks[2 + j // 4][:, (j % 4) * P:(j % 4) * P + NS],
                                    src_f[:, :].rearrange("s (p j) -> s p j", j=TILES)[:, :, j],
                                    ident[0:NS, 0:NS])
            last.then_inc(s_idxT, 1)

            def hist(g, h, start, stop):
                pe.wait_ge(s_hist, g + 1)
                for t in range(HT):
                    last = pe.matmul(banks[7][:, 0:LO], oh_hi[:, h, :, t], oh_lo[:, h, :, t],
                                     start=start and t == 0, stop=stop and t == HT - 1)
                last.then_inc(s_histmm, 1)

            def first_tr(c, n, h, m):
                pe.wait_ge(s_h, c + 1)
                if n == 0:
                    pe.wait_ge(s_srccol, 1)
                if n >= 2:
                    pe.wait_ge(s_hTc, c - 1)
                for k in range(CB):
                    last = pe.transpose(banks[h][:, k * P:(k + 1) * P], z[:, h, k * P:(k + 1) * P], ident[:, :])
                last.then_inc(s_hTp, 1)

            def first_mm(c, n, h, m):
                if n == 0:
                    pe.wait_ge(s_loads, 16 * (N_WEIGHTS + N_BIASES))
                pe.wait_ge(s_hTc, c + 1)
                if n >= 2:
                    pe.wait_ge(s_u, c - 1)
                for k in range(CB):
                    last = pe.matmul(banks[2 + h][:, k * P:(k + 1) * P], hT[:, h, k * P:(k + 1) * P], w1[:, :],
                                     start=True, stop=True)
                last.then_inc(s_hw, 1)

            hist(0, 0, True, False)
            hist(1, 1, False, False)
            with pe.Fori(1, LEAD) as i:
                hist(2 * i, 0, False, False)
                hist(2 * i + 1, 1, False, False)

            def beside(c, n, h, m):
                if n != NCH - 1:
                    hist(2 * c + 2 * LEAD, 0, False, False)
                    hist(2 * c + 2 * LEAD + 1, 1, False, n == NCH - 2)
                first_tr(c, n, h, m)
                if n == NCH - 2:
                    pe.wait_ge(s_halves, 2)
                    for q in range(2):
                        last = pe.matmul(banks[6][:, 0:HI], halves[:, q, :],
                                         ident[0:HV, 0:HV].rearrange("p (k q) -> p q k", q=2)[:, q, :],
                                         start=q == 0, stop=q == 1)
                    last.then_inc(s_count, 1)
            pipeline(pe, (0, beside), (1, first_mm), peel=2)

            def own_rows(c, n, h, m):
                pe.wait_ge(s_own, c + 1)
                if n == 0:
                    pe.wait_ge(s_u, NCH)
                if n >= 2:
                    pe.wait_ge(s_acc0, c - 1)
                for k in range(CB):
                    last = pe.transpose(banks[h][:, k * P:(k + 1) * P], st[:, h, k * P:(k + 1) * P], ident[:, :])
                last.then_inc(s_selfT, 1)
            chunks(pe, own_rows)

            pe.wait_ge(s_span, 1)
            pe.transpose(banks[4][0:1, 0:NS], base_span[:, 0:1], ident[0:NS, 0:NS])
            pe.transpose(banks[4][0:1, P:P + NS], base_span[:, 1:2], ident[0:NS, 0:NS]).then_inc(s_base, 1)
            pe.wait_ge(s_flag, 1)
            pe.matmul(banks[5][0:NS, 0:1], ones[0:1, 0:NS], is_banded[0:1, 0:1], start=True, stop=True).then_inc(s_band, 1)
            pe.wait_ge(s_rel, 1)
            for j in range(TILES):
                last = pe.transpose(banks[4 + j // 4][:, (j % 4) * P:(j % 4) * P + NS],
                                    dst_f[:, :].rearrange("s (p j) -> s p j", j=TILES)[:, :, j],
                                    ident[0:NS, 0:NS])
            last.then_inc(s_relT, 1)

            def broadcasts(ph):
                def broadcast_rows(c, n, h, m):
                    pe.wait_ge(s_diag, ph * NCH + c + 1)
                    if ph or n >= 2:
                        pe.wait_ge(s_dbcc, ph * NCH + (c - 1 if n >= 2 else 0))
                    pe.matmul(banks[2 + h][:, :], ones[:, :], z[:, h], start=True, stop=True).then_inc(s_dbc, 1)
                chunks(pe, broadcast_rows)
            broadcasts(0)

            nwin = pe.value_load(nwin_i[0:1, 0:1], min_val=1, max_val=NW)
            next_supertile = counter(pe, s_started_pe)
            done = pe.alloc_register("windows_pe")
            pe.reg_mov(done, 0)

            def sum_supertile(u, wait):
                wait(0)
                next_supertile()
                with pe.Fori(0, nwin):
                    pe.reg_add(done, done, 1)
                    d = pe.snap(done)
                    pe.wait_ge(s_oh, d)
                    for j in range(TILES):
                        if j == HALF_TILES:
                            wait(1)
                            next_supertile()
                        last = pe.matmul(banks[6 + u % 2][:, 0:W], G[:, u, j, :], oh[:, u % 2, j, :],
                                         start=j == 0, stop=j == TILES - 1)
                    last.then_inc(s_agg, 1)

            def gcn_phase(ph, *steps):
                def body(i, first, last):
                    for u in range(RING):
                        def gathered(half):
                            pe.wait_ge(s_g[u][half], 16 * HALF_TILES * i + 16 * HALF_TILES * (BODIES * ph + 1))
                        sum_supertile(u, gathered)
                gather_loop(pe, body, nwin, steps)

            def second_mm(n, b, h, blocks):
                pe.wait_ge(s_zr, n + 1)
                for k in range(blocks):
                    last = pe.matmul(banks[h][:, k * P:(k + 1) * P], z[:, h, k * P:(k + 1) * P], w2[:, :],
                                     start=True, stop=True)
                last.then_inc(s_zw, 1)

            def second_own(n, b, h, blocks):
                pe.wait_ge(s_t, n + 1)
                for k in range(blocks):
                    last = pe.transpose(banks[2 + h][:, k * P:(k + 1) * P], st[:, h, k * P:(k + 1) * P], ident[:, :])
                last.then_inc(s_selfT, 1)
            gcn_phase(0, second_mm, second_own)
            pe.wait_ge(s_acc0, NCH + UNITS)
            broadcasts(1)

            def third_tr(n, b, h, blocks):
                pe.wait_ge(s_c["z"], n + 1)
                for k in range(blocks):
                    last = pe.transpose(banks[h][:, k * P:(k + 1) * P], z[:, h, k * P:(k + 1) * P], ident[:, :])
                last.then_inc(s_c["tr"], 1)

            def third_hT(n, b, h, blocks):
                pe.wait_ge(s_c["h"], n + 1)
                for k in range(blocks):
                    last = pe.transpose(banks[2 + h][:, k * P:(k + 1) * P], y[:, h, k * P:(k + 1) * P], ident[:, :])
                last.then_inc(s_c["hT"], 1)

            def third_mm(n, b, h, blocks):
                pe.wait_ge(s_c["hTc"], n + 1)
                for k in range(blocks):
                    last = pe.matmul(banks[4 + h][:, k * P:(k + 1) * P], hT[:, h, k * P:(k + 1) * P],
                                     w_node[:, 0:P], start=True, stop=True)
                last.then_inc(s_c["hw"], 1)
            gcn_phase(1, third_tr, third_hT, third_mm)

            def transpose_edges(i, u, n):
                pe.wait_ge(s_e[u], 16 * i + 16)
                for half in range(2):
                    if n >= 1:
                        pe.wait_ge(s_eTc, 2 * RING * i + 2 * u + half - 1)
                    for k in range(4):
                        last = pe.transpose(banks[half][:, k * P:(k + 1) * P], edges[:, u, 4 * half + k, :], ident[:, :])
                    last.then_inc(s_eT, 1)

            def edge_products(i, u, n):
                for half in range(2):
                    m = 2 * RING * i + 2 * u + half
                    pe.wait_ge(s_eTc, m + 1)
                    if n >= 2:
                        pe.wait_ge(s_msum, m - 3)
                    for k in range(4):
                        last = pe.matmul(banks[2 + 2 * (u % 2) + half][:, k * P:(k + 1) * P],
                                         edgeT[:, half, k * P:(k + 1) * P], w_edge[:, :], start=True, stop=True)
                    last.then_inc(s_m, 1)

            pe.wait_ge(s_c["t3"], UNITS)
            pe.wait_ge(s_c["hTa"], UNITS)
            transpose_edges(0, 0, 0)
            edge_products(0, 0, 0)

            def message_body(i, first, last):
                for u in range(RING):
                    if not (last and u == RING - 1):
                        nxt = (i if u < RING - 1 else i + 1, (u + 1) % RING)
                        n = u + 1 if first else 9
                        transpose_edges(*nxt, n)
                        edge_products(*nxt, n)

                    def messages(half):
                        pe.wait_ge(s_msg, 2 * RING * i + 2 * u + half + 1)
                    sum_supertile(u, messages)

            def end_update(n, b, h, blocks):
                pe.wait_ge(s_d["z"], n + 1)
                pe.matmul(end_banks[h][:, 0:blocks * P], w_node[:, P:2 * P], node_cols(hT_all, b, blocks), start=True, stop=False)
                pe.matmul(end_banks[h][:, 0:blocks * P], w_mean[:, :], z[:, h, 0:blocks * P], start=False, stop=True).then_inc(s_d["mm"], 1)

            def end_tr(n, b, h, blocks):
                pe.wait_ge(s_d["u"], n + 1)
                for k in range(blocks):
                    last = pe.transpose(end_banks[h][:, k * P:(k + 1) * P], hT[:, h, k * P:(k + 1) * P], ident[:, :])
                last.then_inc(s_d["tr"], 1)
            gather_loop(pe, message_body, nwin, (end_update, end_tr))

        @block.vector
        def _(dve):
            next_step = counter(dve, s_started_dve)
            dve.wait_ge(s_pool0, 3)
            dve.tensor_copy(iota_hist, bc_free(iota_i[:, 0:VALUES], HT))
            dve.tensor_copy(iota_w[:, :], iota_i[:, 0:W])
            dve.tensor_copy(window_off[:, :], window_i[:, :])
            dve.tensor_copy(least_f[:, :], least_i[:, :])
            dve.memset(count[:, :], 0.0).then_inc(s_iota, 1)
            dve.wait_ge(s_idx[0], 32)
            dve.tensor_copy(dst_f, dst_rows).then_inc(s_dve0, 1)

            dve.wait_ge(s_idxT, 1)
            for b, ps in enumerate(from_psum(0)):
                last = dve.tensor_copy(dst_col.rearrange("p (s j) -> p s j", j=TILES)[:, :, 4 * b:4 * b + 4], ps)
            last.then_inc(s_dstcol, 1)
            dve.wait_ge(s_dstcol, 1)
            dve.tensor_single_scalar(hi_i, dst_col, LO.bit_length() - 1, ALU.arith_shift_right).then_inc(s_split, 1)
            dve.tensor_single_scalar(lo_i, dst_col, LO - 1, ALU.bitwise_and).then_inc(s_split, 1)
            dve.wait_ge(s_split, 2)
            dve.tensor_copy(hi_col, hi_i).then_inc(s_hilo, 1)
            dve.tensor_copy(lo_col, lo_i).then_inc(s_hilo, 1)

            dve.wait_ge(s_iota, 1)
            dve.wait_ge(s_hilo, 2)

            def hist(g, h, wait):
                if wait:
                    dve.wait_ge(s_histmm, g - 1)
                dve.tensor_tensor(oh_lo[:, h], lo_col[:, bass.ds(g * HT, HT)].rearrange("p (o t) -> p o t", o=1).to_broadcast([P, LO, HT]),
                                  iota_hist[:, 0:LO, :], ALU.is_equal)
                dve.tensor_tensor(oh_hi[:, h, 0:HV, :], hi_col[:, bass.ds(g * HT, HT)].rearrange("p (o t) -> p o t", o=1).to_broadcast([P, HV, HT]),
                                  iota_hist[:, 0:HV, :], ALU.is_equal).then_inc(s_hist, 1)
            hist(0, 0, False)
            hist(1, 1, False)
            with dve.Fori(1, LEAD) as i:
                hist(2 * i, 0, True)
                hist(2 * i + 1, 1, True)
            dve.wait_ge(s_std, 1)
            dve.reciprocal(rstd[:, :], rstd[:, :]).then_inc(s_rstd, 1)
            dve.wait_ge(s_rstd, 1)
            dve.tensor_tensor(nmr[:, :], neg_mean[:, :], rstd[:, :], ALU.mult).then_inc(s_rstd, 1)
            with dve.Fori(LEAD, GROUPS // 2) as i:
                hist(2 * i, 0, True)
                hist(2 * i + 1, 1, True)

            dve.wait_ge(s_histmm, GROUPS)
            for q in range(2):
                dve.tensor_copy(halves[:, q, q * LO:(q + 1) * LO], banks[7][0:HV, 0:LO]).then_inc(s_halves, 1)
            dve.wait_ge(s_count, 1)
            dve.tensor_copy(count[:, 0:HI], banks[6][:, 0:HI]).then_inc(s_degree, 1)
            dve.wait_ge(s_degree, 1)
            dve.wait_ge(s_sdeg, 1)
            dve.reciprocal(dinv[:, :], dinv[:, :]).then_inc(s_small, 1)
            dve.wait_ge(s_small, 1)

            def scale_rows(c, n, h, m):
                dve.wait_ge(s_u, c + 1)
                dve.tensor_tensor(chunk_blocks(node_u, c), chunk_blocks(node_u, c), bc_free(dinv[:, bass.ds(c * CB, CB)], P),
                                  ALU.mult).then_inc(s_t1, 1)
            chunks(dve, scale_rows)
            dve.tensor_single_scalar(rcount[:, :], count[:, :], 1.0, ALU.max).then_inc(s_small, 1)

            dve.tensor_reduce(base_span[:, 0:1], dst_f, AX.X, ALU.min).then_inc(s_red, 1)
            dve.wait_ge(s_srccol, 1)
            dve.scalar_tensor_tensor(src_f, dst_f, float(PAD_LIMIT), dst_f,
                                     ALU.is_lt, ALU.mult).then_inc(s_red, 1)
            dve.wait_ge(s_red, 2)
            dve.tensor_reduce(base_used[:, 0:1], src_f, AX.X, ALU.max).then_inc(s_red, 1)
            dve.tensor_scalar(early[:, :], base_span[:, 0:1], least_f[:, 0:1], float(PAD_LIMIT),
                              ALU.is_lt, ALU.mult).then_inc(s_red, 1)
            dve.wait_ge(s_red, 4)
            dve.tensor_tensor(base_used[:, 0:1], base_used[:, 0:1], early[:, 0:1], ALU.add).then_inc(s_red, 1)
            dve.wait_ge(s_red, 5)
            dve.tensor_tensor(base_span[:, 1:2], base_used[:, 0:1], base_span[:, 0:1], ALU.subtract).then_inc(s_span, 1)
            dve.wait_ge(s_small, 2)
            dve.reciprocal(rcount[:, :], rcount[:, :]).then_inc(s_small, 1)
            dve.wait_ge(s_base, 1)
            dve.tensor_reduce(span_max[:, :], banks[4][0:1, P:P + NS], AX.X, ALU.max).then_inc(s_small, 1)
            dve.wait_ge(s_small, 4)
            dve.tensor_single_scalar(is_banded[:, :], span_max[:, :], float(W) - 0.5, ALU.is_lt).then_inc(s_flag, 1)
            dve.wait_ge(s_flag, 1)
            dve.tensor_scalar(nwin_f[:, :], is_banded[:, :], float(1 - NW), float(NW), ALU.mult, ALU.add).then_inc(s_small, 1)
            dve.tensor_scalar(base_row_f[:, :], banks[4][0:1, 0:NS], is_banded[0:1, 0:1], None, ALU.mult).then_inc(s_small, 1)
            dve.wait_ge(s_small, 6)
            dve.tensor_copy(nwin_i[:, :], nwin_f[:, :]).then_inc(s_small, 1)
            dve.tensor_copy(base_row[:, :], base_row_f[:, :]).then_inc(s_small, 1)
            dve.wait_ge(s_band, 1)
            dve.tensor_tensor(base_used[:, :], banks[5][0:NS, 0:1], base_span[:, 0:1], ALU.mult).then_inc(s_red, 1)
            dve.wait_ge(s_red, 6)
            dve.tensor_scalar(dst_f, dst_f, base_used[:, 0:1], None, ALU.subtract).then_inc(s_rel, 1)
            dve.wait_ge(s_relT, 1)
            for b, ps in enumerate(from_psum(4)):
                last = dve.tensor_copy(rel_col[:, :, 4 * b:4 * b + 4], ps)
            last.then_inc(s_relcol, 1)

            def diagonals(ph, value):
                def diagonal(c, n, h, m):
                    if ph or n >= 2:
                        dve.wait_ge(s_dbc, ph * NCH + (c - 1 if n >= 2 else 0))
                    dve.tensor_tensor(q3(z[:, h]), bc_mid(ident[:, :], CB), bc_free(value[:, bass.ds(c * CB, CB)], P),
                                      ALU.mult).then_inc(s_diag, 1)
                chunks(dve, diagonal)

            def add_b2(c, n, h, m):
                dve.tensor_tensor(chunk_blocks(x_sb, c), chunk_blocks(x_sb, c), bc_mid(b2_bc[:, :], CB), ALU.add).then_inc(s_xb, 1)
            diagonals(0, dinv)

            dve.wait_ge(s_small, 8)
            dve.wait_ge(s_relcol, 1)
            nwin = dve.value_load(nwin_i[0:1, 0:1], min_val=1, max_val=NW)
            done = dve.alloc_register("windows_dve")
            dve.reg_mov(done, 0)

            def one_hot(s, k, u):
                dve.scalar_tensor_tensor(oh[:, u % 2], rel_col[:, bass.ds(s, 1), :].rearrange("p s (j o) -> p (s j) o", o=1).to_broadcast([P, TILES, W]),
                                         window_off[:, bass.ds(k, 1)], bc_mid(iota_w[:, :], TILES),
                                         ALU.subtract, ALU.is_equal).then_inc(s_oh, 1)

            def add_window(base, k, u):
                dve.reg_add(done, done, 1)
                d = dve.snap(done)
                start = nc.s_assert_within(base + k * W, 0, NP - W, skip_runtime_bounds_check_because="base is 0 where k is above 0")
                dve.wait_ge(s_agg, d)
                dve.tensor_tensor(acc[:, bass.ds(start, W)], acc[:, bass.ds(start, W)], banks[6 + u % 2][:, 0:W],
                                  ALU.add).then_inc(s_added, 1)
                dve.wait_ge(s_added, d)

            def sum_supertile(i, u, last):
                s = RING * i + u
                base = dve.value_load(base_row[0:1, bass.ds(s, 1)], min_val=0, max_val=N - 1)
                with dve.If(nwin != 1):
                    with dve.Fori(1, nwin) as k:
                        add_window(base, k - 1, u)
                        one_hot(s, k, u)
                if not (last and u == RING - 1):
                    one_hot(s + 1, 0, u + 1)
                add_window(base, nwin - 1, u)
                dve.sem_inc(s_free, 1)

            def gcn_phase(ph, *steps):
                one_hot(0, 0, 0)
                dve.wait_ge(s_acc0, NCH + UNITS * ph)

                def body(i, first, last):
                    for u in range(RING):
                        sum_supertile(i, u, last)
                gather_loop(dve, body, nwin, steps)

            def second_z(n, b, h, blocks):
                dve.tensor_tensor(z[:, h, 0:blocks * P], node_cols(acc, b, blocks), node_cols(dinv_bc, b, blocks), ALU.mult).then_inc(s_z, 1)

            def second_table(n, b, h, blocks):
                dve.wait_ge(s_zw, n + 1)
                if h == 0:
                    dve.wait_ge(s_stored, 16 * n + 16 * NCH)
                    dve.wait_ge(s_selfT, n + NCH)
                dve.tensor_tensor(q3(st[:, h, 0:blocks * P]), q3(banks[h][:, 0:blocks * P]), bc_free(dinv[:, bass.ds(b, blocks)], P),
                                  ALU.mult).then_inc(s_t, 1)
            dve.wait_ge(s_dbcc, NCH)
            gcn_phase(0, second_z, second_table)
            diagonals(1, rcount)
            chunks(dve, add_b2)
            dve.wait_ge(s_dbcc, 2 * NCH)

            def norms(b, sems, rows, h, blocks):
                next_step()
                for k in range(blocks):
                    dve.bn_stats(stats[:, h, k, :], rows(k)).then_inc(sems["bn"], 1)
                dve.wait_ge(sems["bn"], 2 * b + blocks)
                next_step()
                for k in range(blocks):
                    dve.bn_aggr(cmv[:, h, k, :], stats[:, h, k, :]).then_inc(sems["bn"], 1)

            def scales(n, sems, h, blocks):
                dve.wait_ge(sems["std"], n + 1)
                dve.reciprocal(crstd[:, h, 0:blocks], cstd[:, h, 0:blocks]).then_inc(sems["rstd"], 1)
                dve.wait_ge(sems["rstd"], 2 * n + 1)
                dve.scalar_tensor_tensor(cnmr[:, h, 0:blocks], cmv[:, h, 0:blocks, 0], -1.0, crstd[:, h, 0:blocks],
                                         ALU.mult, ALU.mult).then_inc(sems["rstd"], 1)

            def third_z(n, b, h, blocks):
                dve.tensor_tensor(z[:, h, 0:blocks * P], node_cols(acc, b, blocks), node_cols(dinv_bc, b, blocks), ALU.mult).then_inc(s_c["z"], 1)

            def third_x2(n, b, h, blocks):
                dve.wait_ge(s_c["tr"], n + 1)
                dve.tensor_tensor(node_blocks(x_sb, b, blocks), q3(banks[h][:, 0:blocks * P]), node_blocks(x_sb, b, blocks), ALU.add).then_inc(s_c["x2"], 1)
                dve.wait_ge(s_c["x2"], n + 1)
                norms(b, s_c, lambda k: x_sb[:, b + k, :], h, blocks)

            def third_scales(n, b, h, blocks):
                scales(n, s_c, h, blocks)

            def third_kept(n, b, h, blocks):
                dve.wait_ge(s_c["h"], n + 1)
                dve.wait_ge(s_c["z"], n + 1)
                next_step()
                dve.tensor_copy(node_cols(acc, b, blocks), zeros[:, 0:blocks * P]).then_inc(s_c["zero"], 1)
                dve.tensor_tensor(node_blocks(hb_all, b, blocks), q3(y[:, h, 0:blocks * P]), bc_mid(beta_bc[:, :], blocks), ALU.add).then_inc(s_c["hb"], 1)

            def third_table(n, b, h, blocks):
                dve.wait_ge(s_c["hw"], n + 1)
                if h == 0:
                    dve.wait_ge(s_stored, 16 * n + 16 * (NCH + UNITS))
                dve.tensor_tensor(q3(st[:, h, 0:blocks * P]), q3(banks[4 + h][:, 0:blocks * P]), bc_mid(bmsg_bc[:, :], blocks),
                                  ALU.add).then_inc(s_c["t3"], 1)
            gcn_phase(1, third_z, third_x2, third_scales, third_table, third_kept)
            dve.wait_ge(s_c["zero"], UNITS)
            one_hot(0, 0, 0)

            def message_body(i, first, last):
                for u in range(RING):
                    for half in range(2):
                        dve.wait_ge(s_g[u][half], 16 * HALF_TILES * i + 16 * HALF_TILES * (2 * BODIES + 1))
                        dve.wait_ge(s_m, 2 * RING * i + 2 * u + half + 1)
                        rows = G[:, u, 4 * half:4 * half + 4, :]
                        dve.tensor_tensor(rows, q3(banks[2 + 2 * (u % 2) + half][:, :]), rows, ALU.add).then_inc(s_msum, 1)
                    sum_supertile(i, u, last)

            def end_z(n, b, h, blocks):
                dve.tensor_tensor(z[:, h, 0:blocks * P], node_cols(acc, b, blocks), node_cols(rc_bc, b, blocks), ALU.mult).then_inc(s_d["z"], 1)

            def end_norms(n, b, h, blocks):
                dve.wait_ge(s_d["tr"], n + 1)
                norms(b, s_d, lambda k: end_banks[h][:, k * P:(k + 1) * P], h, blocks)

            def end_scales(n, b, h, blocks):
                scales(n, s_d, h, blocks)

            def end_rows(n, b, h, blocks):
                rows, res = [q3(t[:, h, 0:blocks * P]) for t in (st, y)]
                kept, old = [node_blocks(t, b, blocks) for t in (hb_all, x_sb)]
                dve.wait_ge(s_d["n"], n + 1)
                if h == 0:
                    dve.wait_ge(s_stored, 16 * n + 16 * (NCH + 2 * UNITS))
                dve.tensor_tensor(rows, rows, bc_mid(gamma_bc[:, :], blocks), ALU.mult).then_inc(s_d["g"], 1)
                dve.wait_ge(s_d["g"], n + 1)
                dve.tensor_tensor(res, rows, kept, ALU.add).then_inc(s_d["b"], 1)
                dve.wait_ge(s_d["b"], n + 1)
                dve.scalar_tensor_tensor(res, res, 0.0, old, ALU.max, ALU.add).then_inc(s_d["fin"], 1)
            gather_loop(dve, message_body, nwin, (end_z, end_norms, end_scales, end_rows))


_INS = ["x", "src", "dst", "edge_attr_128", "L0_gnn_W1", "L0_gnn_b1", "L0_gnn_W2", "L0_gnn_b2",
        "L1_gnn_W_msg", "L1_gnn_b_msg", "L1_gnn_W_upd", "L1_gnn_b_upd", "L1_gnn_gamma", "L1_gnn_beta"]


def kernel(**inputs):
    import numpy as _np
    import concourse.bacc as _bacc
    from concourse import mybir as _mybir
    from concourse.bass_utils import run_bass_kernel_spmd as _run

    nc = _bacc.Bacc("TRN2", target_bir_lowering=False, num_devices=1)
    arrays, args = {}, []
    for name in _INS:
        a = _np.ascontiguousarray(inputs[name])
        arrays[f"in_{name}"] = a
        args.append(nc.dram_tensor(f"in_{name}", a.shape, _mybir.dt.from_np(a.dtype), kind="ExternalInput").ap())
    shape = inputs["x"].shape
    args.append(nc.dram_tensor("out_x", tuple(shape), _mybir.dt.float32, kind="ExternalOutput").ap())
    gnn_program(nc, *args)
    r = _run(nc, [arrays], core_ids=[0])
    return r.results[0]["out_x"]
```
